# Optimizing a Trainium2 kernel written in Bass

```python
import numpy as np
import jax
import jax.numpy as jnp

def _softmax(x, axis=-1):
    return jax.nn.softmax(x, axis=axis)

def _gelu(x):
    return jax.nn.gelu(x, approximate=True)

def _silu(x):
    return jax.nn.silu(x)

def _sigmoid(x):
    return jax.nn.sigmoid(x)

def _layernorm(x, axis=-1, eps=1e-05):
    m = jnp.mean(x, axis=axis, keepdims=True)
    v = jnp.var(x, axis=axis, keepdims=True)
    return (x - m) / jnp.sqrt(v + eps)

def _scatter_add(tgt, idx, src, axis=0):
    return tgt.at[idx].add(src)

def _segment_sum(src, seg, n):
    return jax.ops.segment_sum(src, seg, n)
kernel_name = 'mk_decoder_preln_d2_seqx_r4_00a3cb'

def setup_inputs(seed: int=0):
    np.random.seed(seed)
    _w = jnp.asarray

    def _rec_inputs():
        import jax
        import jax.numpy as jnp
        _rk = jax.random.key(seed)
        x = 0.002226 + 0.9996 * jax.random.normal(jax.random.fold_in(_rk, 1), (4, 512, 256), jnp.float32)
        _lenS = 512 - jax.random.randint(jax.random.fold_in(_rk, 7), (4,), 0, max(1, 512 // 4) + 1, jnp.int32)
        _lenS2 = 1024 - jax.random.randint(jax.random.fold_in(_rk, 8), (4,), 0, max(1, 1024 // 4) + 1, jnp.int32)
        _ctx_1024P = jax.random.normal(jax.random.fold_in(_rk, 11), (4, 16, 256), jnp.float32)
        _ctx_1024c = jax.random.dirichlet(jax.random.fold_in(_rk, 511), 0.3 * jnp.ones((16,), jnp.float32), (4, 1024))
        _ctx_1024t = jnp.einsum('bsk,bkd->bsd', _ctx_1024c, _ctx_1024P)
        _ctx_1024t = _ctx_1024t * jax.lax.rsqrt(jnp.mean(jnp.square(_ctx_1024t)) + 1e-12) * 0.953939
        ctx_1024 = -0.000125008 + 0.999885 * (_ctx_1024t + 0.3 * jax.random.normal(jax.random.fold_in(_rk, 611), (4, 1024, 256), jnp.float32))
        return (x, ctx_1024)
    x, ctx_1024 = _rec_inputs()

    def _L0_attn_setup():
        import jax, jax.numpy as jnp
        import numpy as np
        B, S, D = (8, 1024, 256)
        WIN = 257
        HALF = WIN // 2
        BL = 64

        def _blockify(t, nb):
            b, s, d = t.shape
            tp = jnp.pad(t, ((0, 0), (BL, BL), (0, 0)))
            tb = tp.reshape(b, nb + 2, BL, d)
            return jnp.concatenate([tb[:, :-2], tb[:, 1:-1], tb[:, 2:]], axis=2)

        def _local_attention(q, k, v):
            b, s, d = q.shape
            nb = s // BL
            qb = q.reshape(b, nb, BL, d)
            kb = _blockify(k, nb)
            vb = _blockify(v, nb)
            scale = 1.0 / np.sqrt(d).astype(np.float32)
            scores = jnp.einsum('bnqd,bnkd->bnqk', qb, kb) * scale
            blk = jnp.arange(nb)[:, None, None]
            r = jnp.arange(BL)[None, :, None]
            c = jnp.arange(3 * BL)[None, None, :]
            i = blk * BL + r
            j = (blk - 1) * BL + c
            rel = j - i
            valid = (rel >= -HALF) & (rel <= HALF) & (j >= 0) & (j < s)
            scores = jnp.where(valid[None], scores, -jnp.inf)
            weights = jax.nn.softmax(scores, axis=-1)
            out = jnp.einsum('bnqk,bnkd->bnqd', weights, vb)
            return out.reshape(b, s, d)
        key = jax.random.key(seed)
        ks = jax.random.split(key, 7)
        s = 0.02
        return {'x': jax.random.normal(ks[0], (B, S, D), jnp.float32), 'Wq': jax.random.normal(ks[1], (D, D), jnp.float32) * s, 'bq': jnp.zeros((D,), jnp.float32), 'Wk': jax.random.normal(ks[2], (D, D), jnp.float32) * s, 'bk': jnp.zeros((D,), jnp.float32), 'Wv': jax.random.normal(ks[3], (D, D), jnp.float32) * s, 'bv': jnp.zeros((D,), jnp.float32)}
    _L0_attn_all = _L0_attn_setup()
    _L0_attn_in = {k: v for k, v in _L0_attn_all.items() if k in ('Wq', 'bq', 'Wk', 'bk', 'Wv', 'bv')}
    del _L0_attn_all

    def _L0_xattn_setup():
        import jax, jax.numpy as jnp
        import numpy as np
        B, M, N, DIM, DH, H = (8, 1024, 64, 256, 128, 8)
        INNER = DH * H
        EPS = 1e-05

        def _layernorm(x, g, b):
            mu = jnp.mean(x, axis=-1, keepdims=True)
            var = jnp.var(x, axis=-1, keepdims=True)
            return (x - mu) * jax.lax.rsqrt(var + EPS) * g + b
        key = jax.random.key(seed)
        ks = jax.random.split(key, 8)
        sd = 0.02
        return {'x': jax.random.normal(ks[0], (B, M, DIM), jnp.float32), 'latents': jax.random.normal(ks[1], (B, N, DIM), jnp.float32), 'gamma_media': jnp.ones((DIM,), jnp.float32), 'beta_media': jnp.zeros((DIM,), jnp.float32), 'gamma_lat': jnp.ones((DIM,), jnp.float32), 'beta_lat': jnp.zeros((DIM,), jnp.float32), 'Wq': jax.random.normal(ks[2], (DIM, INNER), jnp.float32) * sd, 'bq': jnp.zeros((INNER,), jnp.float32), 'Wkv': jax.random.normal(ks[3], (DIM, 2 * INNER), jnp.float32) * sd, 'bkv': jnp.zeros((2 * INNER,), jnp.float32), 'Wo': jax.random.normal(ks[4], (INNER, DIM), jnp.float32) * sd, 'bo': jnp.zeros((DIM,), jnp.float32)}
    _L0_xattn_all = _L0_xattn_setup()
    _L0_xattn_in = {k: v for k, v in _L0_xattn_all.items() if k in ('gamma_media', 'beta_media', 'gamma_lat', 'beta_lat', 'Wq', 'bq', 'Wkv', 'bkv', 'Wo', 'bo')}
    del _L0_xattn_all

    def _L0_ffn_setup():
        import jax, jax.numpy as jnp
        import numpy as np
        B, S, D_MODEL, D_HIDDEN = (4, 512, 256, 1024)

        def act_quant(x):
            scale = 127.0 / jnp.clip(jnp.max(jnp.abs(x), axis=-1, keepdims=True), 1e-05)
            return jnp.clip(jnp.round(x * scale), -128, 127) / scale

        def weight_quant(w):
            scale = 1.0 / jnp.clip(jnp.mean(jnp.abs(w)), 1e-05)
            return jnp.clip(jnp.round(w * scale), -1, 1) / scale

        def bit_linear(x, w):
            xq = x + jax.lax.stop_gradient(act_quant(x) - x)
            wq = w + jax.lax.stop_gradient(weight_quant(w) - w)
            return jnp.einsum('bsd,hd->bsh', xq, wq)

        def depthwise_conv1d(x_bcl, w, b):
            y = jax.lax.conv_general_dilated(x_bcl, w, window_strides=(1,), padding=[(1, 1)], dimension_numbers=('NCH', 'OIH', 'NCH'), feature_group_count=x_bcl.shape[1])
            return y + b[None, :, None]
        key = jax.random.key(seed)
        ks = jax.random.split(key, 5)
        lim1 = 1.0 / np.sqrt(D_MODEL)
        lim2 = 1.0 / np.sqrt(D_HIDDEN)
        limc = 1.0 / np.sqrt(3.0)
        return {'x': jax.random.normal(ks[0], (B, S, D_MODEL), dtype=jnp.float32), 'w1': jax.random.uniform(ks[1], (D_HIDDEN, D_MODEL), jnp.float32, -lim1, lim1), 'conv_w': jax.random.uniform(ks[2], (D_HIDDEN, 1, 3), jnp.float32, -limc, limc), 'conv_b': jax.random.uniform(ks[3], (D_HIDDEN,), jnp.float32, -limc, limc), 'w2': jax.random.uniform(ks[4], (D_MODEL, D_HIDDEN), jnp.float32, -lim2, lim2)}
    _L0_ffn_all = _L0_ffn_setup()
    _L0_ffn_in = {k: v for k, v in _L0_ffn_all.items() if k in ('w1', 'conv_w', 'conv_b', 'w2')}
    del _L0_ffn_all

    def _L1_attn_setup():
        import jax, jax.numpy as jnp
        import numpy as np
        INDIM = 256
        NHEADS = 16
        DK = INDIM // NHEADS
        DV = INDIM // NHEADS
        B, S = (4, 512)
        key = jax.random.key(seed)
        ks = jax.random.split(key, 5)
        x = jax.random.normal(ks[0], (B, S, INDIM), dtype=jnp.float32)
        std_qk = np.sqrt(2.0 / (INDIM + DK)).astype(np.float32)
        std_v = np.sqrt(2.0 / (INDIM + DV)).astype(np.float32)
        Wq = jax.random.normal(ks[1], (NHEADS * DK, INDIM), dtype=jnp.float32) * std_qk
        Wk = jax.random.normal(ks[2], (NHEADS * DK, INDIM), dtype=jnp.float32) * std_qk
        Wv = jax.random.normal(ks[3], (NHEADS * DV, INDIM), dtype=jnp.float32) * std_v
        std_o = np.sqrt(2.0 / (NHEADS * DV + INDIM)).astype(np.float32)
        Wo = jax.random.normal(ks[4], (INDIM, NHEADS * DV), dtype=jnp.float32) * std_o
        bq = jnp.zeros((NHEADS * DK,), jnp.float32)
        bk = jnp.zeros((NHEADS * DK,), jnp.float32)
        bv = jnp.zeros((NHEADS * DV,), jnp.float32)
        bo = jnp.zeros((INDIM,), jnp.float32)
        return {'x': x, 'Wq': Wq, 'bq': bq, 'Wk': Wk, 'bk': bk, 'Wv': Wv, 'bv': bv, 'Wo': Wo, 'bo': bo}
    _L1_attn_all = _L1_attn_setup()
    _L1_attn_in = {k: v for k, v in _L1_attn_all.items() if k in ('Wq', 'bq', 'Wk', 'bk', 'Wv', 'bv', 'Wo', 'bo')}
    del _L1_attn_all

    def _L1_xattn_setup():
        import jax, jax.numpy as jnp
        import numpy as np
        DIM = 256
        N_HEADS = 16
        HEAD_DIM = DIM // N_HEADS
        GAMMA = 10.0

        def larope_cos_sin(seq_len, gamma, head_dim):
            inv_freq = 1.0 / 10000.0 ** (jnp.arange(0, head_dim, 2, dtype=jnp.float32) / head_dim)
            t = jnp.arange(seq_len, dtype=jnp.float32)
            freqs = jnp.outer(gamma * (t / seq_len), inv_freq)
            emb = jnp.concatenate([freqs, freqs], axis=-1)
            return (jnp.cos(emb), jnp.sin(emb))

        def apply_rope(x, cos, sin):
            d = x.shape[-1] // 2
            x1, x2 = (x[..., :d], x[..., d:])
            c = cos[None, None, :, :d]
            s = sin[None, None, :, :d]
            return jnp.concatenate([x1 * c - x2 * s, x1 * s + x2 * c], axis=-1)
        key = jax.random.key(seed)
        ks = jax.random.split(key, 11)
        B, Lq, Lk = (4, 512, 256)
        std = 1.0 / np.sqrt(DIM)
        inp = {'query': jax.random.normal(ks[0], (B, Lq, DIM), dtype=jnp.float32), 'key': jax.random.normal(ks[1], (B, Lk, DIM), dtype=jnp.float32), 'value': jax.random.normal(ks[2], (B, Lk, DIM), dtype=jnp.float32), 'Wq': jax.random.normal(ks[3], (DIM, DIM), dtype=jnp.float32) * std, 'bq': jnp.zeros((DIM,), dtype=jnp.float32), 'Wk': jax.random.normal(ks[4], (DIM, DIM), dtype=jnp.float32) * std, 'bk': jnp.zeros((DIM,), dtype=jnp.float32), 'Wv': jax.random.normal(ks[5], (DIM, DIM), dtype=jnp.float32) * std, 'bv': jnp.zeros((DIM,), dtype=jnp.float32), 'Wo': jax.random.normal(ks[6], (DIM, DIM), dtype=jnp.float32) * std, 'bo': jnp.zeros((DIM,), dtype=jnp.float32)}
        return inp
    _L1_xattn_all = _L1_xattn_setup()
    _L1_xattn_in = {k: v for k, v in _L1_xattn_all.items() if k in ('Wq', 'bq', 'Wk', 'bk', 'Wv', 'bv', 'Wo', 'bo')}
    del _L1_xattn_all

    def _L1_ffn_setup():
        import jax, jax.numpy as jnp
        import numpy as np
        H = 256
        I = 256
        E = 8
        key = jax.random.key(seed)
        ks = jax.random.split(key, 8)
        s = 0.02
        x = jax.random.normal(ks[0], (4, 512, H), dtype=jnp.float32)
        Wg = jax.random.normal(ks[1], (H, E), dtype=jnp.float32) * s
        bg = jnp.zeros((E,), dtype=jnp.float32)
        W1 = jax.random.normal(ks[2], (E, H, I), dtype=jnp.float32) * s
        b1 = jnp.zeros((E, I), dtype=jnp.float32)
        W2 = jax.random.normal(ks[3], (E, I, H), dtype=jnp.float32) * s
        b2 = jnp.zeros((E, H), dtype=jnp.float32)
        return {'x': x, 'Wg': Wg, 'bg': bg, 'W1': W1, 'b1': b1, 'W2': W2, 'b2': b2}
    _L1_ffn_all = _L1_ffn_setup()
    _L1_ffn_in = {k: v for k, v in _L1_ffn_all.items() if k in ('Wg', 'bg', 'W1', 'b1', 'W2', 'b2')}
    del _L1_ffn_all
    return {'x': x, 'ctx_1024': ctx_1024, 'L0_attn_Wq': _L0_attn_in['Wq'], 'L0_attn_bq': _L0_attn_in['bq'], 'L0_attn_Wk': _L0_attn_in['Wk'], 'L0_attn_bk': _L0_attn_in['bk'], 'L0_attn_Wv': _L0_attn_in['Wv'], 'L0_attn_bv': _L0_attn_in['bv'], 'L0_xattn_gamma_media': _L0_xattn_in['gamma_media'], 'L0_xattn_beta_media': _L0_xattn_in['beta_media'], 'L0_xattn_gamma_lat': _L0_xattn_in['gamma_lat'], 'L0_xattn_beta_lat': _L0_xattn_in['beta_lat'], 'L0_xattn_Wq': _L0_xattn_in['Wq'], 'L0_xattn_bq': _L0_xattn_in['bq'], 'L0_xattn_Wkv': _L0_xattn_in['Wkv'], 'L0_xattn_bkv': _L0_xattn_in['bkv'], 'L0_xattn_Wo': _L0_xattn_in['Wo'], 'L0_xattn_bo': _L0_xattn_in['bo'], 'L0_ffn_w1': _L0_ffn_in['w1'], 'L0_ffn_conv_w': _L0_ffn_in['conv_w'], 'L0_ffn_conv_b': _L0_ffn_in['conv_b'], 'L0_ffn_w2': _L0_ffn_in['w2'], 'L1_attn_Wq': _L1_attn_in['Wq'], 'L1_attn_bq': _L1_attn_in['bq'], 'L1_attn_Wk': _L1_attn_in['Wk'], 'L1_attn_bk': _L1_attn_in['bk'], 'L1_attn_Wv': _L1_attn_in['Wv'], 'L1_attn_bv': _L1_attn_in['bv'], 'L1_attn_Wo': _L1_attn_in['Wo'], 'L1_attn_bo': _L1_attn_in['bo'], 'L1_xattn_Wq': _L1_xattn_in['Wq'], 'L1_xattn_bq': _L1_xattn_in['bq'], 'L1_xattn_Wk': _L1_xattn_in['Wk'], 'L1_xattn_bk': _L1_xattn_in['bk'], 'L1_xattn_Wv': _L1_xattn_in['Wv'], 'L1_xattn_bv': _L1_xattn_in['bv'], 'L1_xattn_Wo': _L1_xattn_in['Wo'], 'L1_xattn_bo': _L1_xattn_in['bo'], 'L1_ffn_Wg': _L1_ffn_in['Wg'], 'L1_ffn_bg': _L1_ffn_in['bg'], 'L1_ffn_W1': _L1_ffn_in['W1'], 'L1_ffn_b1': _L1_ffn_in['b1'], 'L1_ffn_W2': _L1_ffn_in['W2'], 'L1_ffn_b2': _L1_ffn_in['b2']}

def reference(x, ctx_1024, L0_attn_Wq, L0_attn_bq, L0_attn_Wk, L0_attn_bk, L0_attn_Wv, L0_attn_bv, L0_xattn_gamma_media, L0_xattn_beta_media, L0_xattn_gamma_lat, L0_xattn_beta_lat, L0_xattn_Wq, L0_xattn_bq, L0_xattn_Wkv, L0_xattn_bkv, L0_xattn_Wo, L0_xattn_bo, L0_ffn_w1, L0_ffn_conv_w, L0_ffn_conv_b, L0_ffn_w2, L1_attn_Wq, L1_attn_bq, L1_attn_Wk, L1_attn_bk, L1_attn_Wv, L1_attn_bv, L1_attn_Wo, L1_attn_bo, L1_xattn_Wq, L1_xattn_bq, L1_xattn_Wk, L1_xattn_bk, L1_xattn_Wv, L1_xattn_bv, L1_xattn_Wo, L1_xattn_bo, L1_ffn_Wg, L1_ffn_bg, L1_ffn_W1, L1_ffn_b1, L1_ffn_W2, L1_ffn_b2):
    import jax
    import jax.numpy as jnp

    def _L0_attn_ref(x, Wq, bq, Wk, bk, Wv, bv):
        import jax, jax.numpy as jnp
        import numpy as np
        B, S, D = (8, 1024, 256)
        WIN = 257
        HALF = WIN // 2
        BL = 64

        def _blockify(t, nb):
            b, s, d = t.shape
            tp = jnp.pad(t, ((0, 0), (BL, BL), (0, 0)))
            tb = tp.reshape(b, nb + 2, BL, d)
            return jnp.concatenate([tb[:, :-2], tb[:, 1:-1], tb[:, 2:]], axis=2)

        def _local_attention(q, k, v):
            b, s, d = q.shape
            nb = s // BL
            qb = q.reshape(b, nb, BL, d)
            kb = _blockify(k, nb)
            vb = _blockify(v, nb)
            scale = 1.0 / np.sqrt(d).astype(np.float32)
            scores = jnp.einsum('bnqd,bnkd->bnqk', qb, kb) * scale
            blk = jnp.arange(nb)[:, None, None]
            r = jnp.arange(BL)[None, :, None]
            c = jnp.arange(3 * BL)[None, None, :]
            i = blk * BL + r
            j = (blk - 1) * BL + c
            rel = j - i
            valid = (rel >= -HALF) & (rel <= HALF) & (j >= 0) & (j < s)
            scores = jnp.where(valid[None], scores, -jnp.inf)
            weights = jax.nn.softmax(scores, axis=-1)
            out = jnp.einsum('bnqk,bnkd->bnqd', weights, vb)
            return out.reshape(b, s, d)
        q = x @ Wq + bq
        k = x @ Wk + bk
        v = x @ Wv + bv
        return _local_attention(q, k, v)

    def _L0_xattn_ref(x, latents, gamma_media, beta_media, gamma_lat, beta_lat, Wq, bq, Wkv, bkv, Wo, bo):
        import jax, jax.numpy as jnp
        import numpy as np
        B, M, N, DIM, DH, H = (8, 1024, 64, 256, 128, 8)
        INNER = DH * H
        EPS = 1e-05

        def _layernorm(x, g, b):
            mu = jnp.mean(x, axis=-1, keepdims=True)
            var = jnp.var(x, axis=-1, keepdims=True)
            return (x - mu) * jax.lax.rsqrt(var + EPS) * g + b
        b = x.shape[0]
        xn = _layernorm(x, gamma_media, beta_media)
        ln = _layernorm(latents, gamma_lat, beta_lat)
        q = ln @ Wq + bq
        kv_input = jnp.concatenate([xn, ln], axis=1)
        kv = kv_input @ Wkv + bkv
        k, v = jnp.split(kv, 2, axis=-1)

        def to_heads(t):
            return t.reshape(b, t.shape[1], H, DH).transpose(0, 2, 1, 3)
        q, k, v = (to_heads(q), to_heads(k), to_heads(v))
        q = q * DH ** (-0.5)
        sim = jnp.einsum('bhid,bhjd->bhij', q, k)
        attn = jax.nn.softmax(sim, axis=-1)
        out = jnp.einsum('bhij,bhjd->bhid', attn, v)
        out = out.transpose(0, 2, 1, 3).reshape(b, -1, INNER)
        return out @ Wo + bo

    def _L0_ffn_ref(x, w1, conv_w, conv_b, w2):
        import jax, jax.numpy as jnp
        import numpy as np
        B, S, D_MODEL, D_HIDDEN = (4, 512, 256, 1024)

        def act_quant(x):
            scale = 127.0 / jnp.clip(jnp.max(jnp.abs(x), axis=-1, keepdims=True), 1e-05)
            return jnp.clip(jnp.round(x * scale), -128, 127) / scale

        def weight_quant(w):
            scale = 1.0 / jnp.clip(jnp.mean(jnp.abs(w)), 1e-05)
            return jnp.clip(jnp.round(w * scale), -1, 1) / scale

        def bit_linear(x, w):
            xq = x + jax.lax.stop_gradient(act_quant(x) - x)
            wq = w + jax.lax.stop_gradient(weight_quant(w) - w)
            return jnp.einsum('bsd,hd->bsh', xq, wq)

        def depthwise_conv1d(x_bcl, w, b):
            y = jax.lax.conv_general_dilated(x_bcl, w, window_strides=(1,), padding=[(1, 1)], dimension_numbers=('NCH', 'OIH', 'NCH'), feature_group_count=x_bcl.shape[1])
            return y + b[None, :, None]
        h = bit_linear(x, w1)
        h = depthwise_conv1d(h.transpose(0, 2, 1), conv_w, conv_b)
        h = h.transpose(0, 2, 1)
        h = jax.nn.silu(h)
        return bit_linear(h, w2)

    def _L1_attn_ref(x, Wq, bq, Wk, bk, Wv, bv, Wo, bo):
        import jax, jax.numpy as jnp
        import numpy as np
        INDIM = 256
        NHEADS = 16
        DK = INDIM // NHEADS
        DV = INDIM // NHEADS
        B, S = (4, 512)
        b, s, _ = x.shape
        q = (x @ Wq.T + bq).reshape(b, s, NHEADS, DK)
        k = (x @ Wk.T + bk).reshape(b, s, NHEADS, DK)
        v = (x @ Wv.T + bv).reshape(b, s, NHEADS, DV)
        w = jnp.einsum('bshd,bzhd->bhsz', q, k)
        w = w / jnp.sqrt(jnp.float32(DV))
        w = jax.nn.softmax(w, axis=-1)
        vw = jnp.einsum('bhsz,bzhd->bshd', w, v)
        vw = vw.reshape(b, s, NHEADS * DV)
        out = vw @ Wo.T + bo
        return out

    def _L1_xattn_ref(query, key, value, Wq, bq, Wk, bk, Wv, bv, Wo, bo):
        import jax, jax.numpy as jnp
        import numpy as np
        DIM = 256
        N_HEADS = 16
        HEAD_DIM = DIM // N_HEADS
        GAMMA = 10.0

        def larope_cos_sin(seq_len, gamma, head_dim):
            inv_freq = 1.0 / 10000.0 ** (jnp.arange(0, head_dim, 2, dtype=jnp.float32) / head_dim)
            t = jnp.arange(seq_len, dtype=jnp.float32)
            freqs = jnp.outer(gamma * (t / seq_len), inv_freq)
            emb = jnp.concatenate([freqs, freqs], axis=-1)
            return (jnp.cos(emb), jnp.sin(emb))

        def apply_rope(x, cos, sin):
            d = x.shape[-1] // 2
            x1, x2 = (x[..., :d], x[..., d:])
            c = cos[None, None, :, :d]
            s = sin[None, None, :, :d]
            return jnp.concatenate([x1 * c - x2 * s, x1 * s + x2 * c], axis=-1)
        B, Lq, _ = query.shape
        Lk = key.shape[1]
        scale = HEAD_DIM ** (-0.5)

        def proj(x, W, b, L):
            y = x @ W.T + b
            return y.reshape(B, L, N_HEADS, HEAD_DIM).transpose(0, 2, 1, 3)
        q = proj(query, Wq, bq, Lq)
        k = proj(key, Wk, bk, Lk)
        v = proj(value, Wv, bv, Lk)
        q_cos, q_sin = larope_cos_sin(Lq, GAMMA, HEAD_DIM)
        k_cos, k_sin = larope_cos_sin(Lk, GAMMA, HEAD_DIM)
        q = apply_rope(q, q_cos, q_sin)
        k = apply_rope(k, k_cos, k_sin)
        scores = jnp.einsum('bhqd,bhkd->bhqk', q, k) * scale
        attn = jax.nn.softmax(scores, axis=-1)
        out = jnp.einsum('bhqk,bhkd->bhqd', attn, v)
        out = out.transpose(0, 2, 1, 3).reshape(B, Lq, DIM)
        return out @ Wo.T + bo

    def _L1_ffn_ref(x, Wg, bg, W1, b1, W2, b2):
        import jax, jax.numpy as jnp
        import numpy as np
        H = 256
        I = 256
        E = 8
        B, S, Hd = x.shape
        xf = x.reshape(-1, Hd)
        logits = xf @ Wg + bg
        gates = jax.nn.softmax(logits, axis=-1)
        idx = jnp.argmax(gates, axis=-1)
        h = jax.nn.gelu(jnp.einsum('th,ehi->tei', xf, W1) + b1, approximate=False)
        y = jnp.einsum('tei,eih->teh', h, W2) + b2
        out = jnp.take_along_axis(y, idx[:, None, None], axis=1)[:, 0, :]
        return out.reshape(B, S, Hd)
    x = x + _L0_attn_ref(_layernorm(x, axis=-1), L0_attn_Wq, L0_attn_bq, L0_attn_Wk, L0_attn_bk, L0_attn_Wv, L0_attn_bv)
    x = x + _L0_xattn_ref(ctx_1024, _layernorm(x, axis=-1), L0_xattn_gamma_media, L0_xattn_beta_media, L0_xattn_gamma_lat, L0_xattn_beta_lat, L0_xattn_Wq, L0_xattn_bq, L0_xattn_Wkv, L0_xattn_bkv, L0_xattn_Wo, L0_xattn_bo)
    x = x + _L0_ffn_ref(_layernorm(x, axis=-1), L0_ffn_w1, L0_ffn_conv_w, L0_ffn_conv_b, L0_ffn_w2)
    x = x + _L1_attn_ref(_layernorm(x, axis=-1), L1_attn_Wq, L1_attn_bq, L1_attn_Wk, L1_attn_bk, L1_attn_Wv, L1_attn_bv, L1_attn_Wo, L1_attn_bo)
    x = x + _L1_xattn_ref(_layernorm(x, axis=-1), ctx_1024, ctx_1024, L1_xattn_Wq, L1_xattn_bq, L1_xattn_Wk, L1_xattn_bk, L1_xattn_Wv, L1_xattn_bv, L1_xattn_Wo, L1_xattn_bo)
    x = x + _L1_ffn_ref(_layernorm(x, axis=-1), L1_ffn_Wg, L1_ffn_bg, L1_ffn_W1, L1_ffn_b1, L1_ffn_W2, L1_ffn_b2)
    return x

_drawn_inputs = setup_inputs


def setup_inputs(seed=0):
    import zlib

    import numpy as np

    out = dict(_drawn_inputs(seed))
    spreads = {'L0_attn_bq': (0.0, 0.8),
     'L0_attn_bk': (0.0, 0.8),
     'L0_attn_bv': (0.0, 0.1),
     'L0_xattn_gamma_media': (1.0, 0.575),
     'L0_xattn_beta_media': (0.0, 0.347),
     'L0_xattn_gamma_lat': (1.0, 0.6),
     'L0_xattn_beta_lat': (0.0, 0.596),
     'L0_xattn_bq': (0.0, 0.8),
     'L0_xattn_bkv': (0.0, 0.1),
     'L0_xattn_bo': (0.0, 0.1),
     'L1_attn_bq': (0.0, 0.1),
     'L1_attn_bk': (0.0, 0.8),
     'L1_attn_bv': (0.0, 0.1),
     'L1_attn_bo': (0.0, 0.1),
     'L1_xattn_bq': (0.0, 0.38),
     'L1_xattn_bk': (0.0, 0.8),
     'L1_xattn_bv': (0.0, 0.1),
     'L1_xattn_bo': (0.0, 0.1),
     'L1_ffn_bg': (0.0, 0.1),
     'L1_ffn_b1': (0.0, 0.531),
     'L1_ffn_b2': (0.0, 0.1)}
    factors = {'L0_attn_Wq': 7.704, 'L0_attn_Wk': 6.267, 'L0_xattn_Wq': 8.0}
    for name, (base, spread) in spreads.items():
        noise = np.random.default_rng([zlib.crc32(name.encode()), seed]).standard_normal(out[name].shape)
        drawn = base * np.exp(spread * noise) if base else spread * noise
        out[name] = jnp.asarray(drawn.astype(out[name].dtype))
    for name, factor in factors.items():
        out[name] = (out[name] * factor).astype(out[name].dtype)
    return out
```

```python
import concourse.bass as bass
import numpy as np
from concourse import mybir
from contextlib import ExitStack

F32 = mybir.dt.float32
F16 = mybir.dt.float16
ALU = mybir.AluOpType
ACT = mybir.ActivationFunctionType
AX = mybir.AxisListType

B, S, D = 4, 512, 256
NCTX = 1024
P = 128
NT = S // P
DC = D // P
HID = 1024
NM = HID // P
XH, XD = 8, 128
XIN = XH * XD
NKV = NCTX + S
KT_TILES = NKV // P
LH, LD = 16, 16
KR = 96
NE = 8
OWN_PER_BATCH = 205
BL = 64
ROUND = 1.5 * 2.0 ** 23

RESIDENT = [("aq", DC, D), ("ak", DC, D), ("av", DC, D), ("xq", DC, XIN), ("xkv", DC, 2 * XIN),
            ("xo", XH, D), ("sq", DC, D), ("sk", DC, D), ("sv", DC, D), ("so", DC, D),
            ("cq", DC, D), ("cqs", DC, D), ("ck", DC, D), ("cks", DC, D), ("cv", DC, D),
            ("co", DC, D), ("g", DC, NE)]
OFF, _n = {}, 0
for _name, _c, _w in RESIDENT:
    OFF[_name] = _n
    _n += _c * _w
NW = _n
WCH = 8
assert NW % WCH == 0
WC = NW // WCH
EW = 2 * DC * D

COL, _n = {}, 0
for _name, _w in [("abq", DC), ("abk", DC), ("xbq", XH), ("xbk", XH), ("xbv", XH), ("gm", DC),
                  ("bm", DC), ("gl", DC), ("bl", DC), ("cw", 3 * NM), ("cb", NM), ("sbq", DC),
                  ("sbk", DC), ("sbv", DC), ("cbq", DC), ("cbqs", DC), ("cbk", DC),
                  ("cbks", DC), ("cbv", DC), ("b1", NE * DC), ("half", 4)]:
    COL[_name] = _n
    _n += _w
NCOL = _n
ROW, _n = {}, 0
for _name, _w in [("abv", D), ("xbo", D), ("sbo", D), ("cbo", D), ("bg", NE), ("order", NE)]:
    ROW[_name] = _n
    _n += _w
NROW = _n


class Signal:

    def __init__(self, nc, ctx, name, per_batch=0, credit=0):
        self.sem = ctx.enter_context(nc.semaphore(name))
        self.per_batch, self.credit = per_batch, credit

    def at(self, b, n):
        return b * self.per_batch + n + self.credit


class Order:

    def __init__(self, eng, sem):
        self.eng, self.sem, self.n, self.base, self.open = eng, sem, 0, 0, []

    def mark(self, ins):
        self.n += 1
        ins.then_inc(self.sem, 1)

    def wait(self):
        self.eng.wait_ge(self.sem, self.base + self.n)

    def link(self, ins):
        self.mark(ins)
        self.wait()

    def enter(self, i, first, per_turn):
        self.open.append((self.n, self.base, per_turn))
        self.base = self.base + (i - first) * per_turn

    def leave(self, turns):
        n, base, per_turn = self.open.pop()
        assert self.n - n == per_turn, (self.n - n, per_turn)
        self.n, self.base = n + per_turn * turns, base


def decoder(nc, x_dram, ctx_dram, ctxT_dram, w_dram, moe_in, tern_in, col_in, row_in, b2_in, mask_in,
            rope_q_in, rope_k_in, ident_in, ident16_in, out):
    c_ = ExitStack()
    with c_:
        def sb(name, shape, dt=F32):
            return c_.enter_context(nc.sbuf_tensor(name, shape, dt))

        def sig(name, per_batch=0, credit=0):
            return Signal(nc, c_, name, per_batch, credit)

        wh, wl = sb("wh", [P, NW], F16), sb("wl", [P, NW], F16)
        tern = sb("tern", [P, 2, DC * HID], F16)
        x = sb("x", [P, NT, D])
        y = sb("y", [P, NT, D])
        y_pad = (sb("yT_hi", [P, DC, S + 2 * BL], F16), sb("yT_lo", [P, DC, S + 2 * BL], F16))
        yT = tuple(t[:, :, BL:BL + S] for t in y_pad)
        akT_pad = (sb("akT_hi", [P, DC, S + 2 * BL], F16), sb("akT_lo", [P, DC, S + 2 * BL], F16))
        col = sb("col", [P, NCOL])
        row = sb("row", [P, NROW])
        b2 = sb("b2", [NE, D])
        b2h, b2l = sb("b2h", [NE, D], F16), sb("b2l", [NE, D], F16)
        mask = sb("mask", [P, 4, 2 * P])
        rope_q = sb("rope_q", [P, 2, S])
        rope_k = sb("rope_k", [P, 2, NCTX])
        ident = sb("ident", [P, P])
        ident16 = sb("ident16", [P, P], F16)
        ones = sb("ones", [P, P])
        st = sb("st", [P, NT, 6])
        mv = sb("mv", [P, NT, 2])
        ve = sb("ve", [P, NT])
        rstd = sb("rstd", [P, NT])
        quant = sb("quant", [P, 2, 4, NT])
        wsum = sb("wsum", [P, 2])
        mw = sb("mw", [P, 2])
        msc = sb("msc", [P, 2])
        nm = sb("nm", [P, 8])
        sums = sb("sums", [P, 4])
        rs = sb("rs", [P, 4])
        rl = sb("rl", [P, NT * LH])

        ARENA = 97 * 1024
        arena = sb("arena", [P, ARENA // 4])

        class Layout:
            def __init__(self, at=0):
                self.at = at

            def take(self, shape, dt=F32):
                n = int(np.prod(shape)) * (4 if dt == F32 else 2)
                assert n % 4 == 0 and self.at + n <= ARENA, (self.at, n)
                v = arena[:, self.at // 4:(self.at + n) // 4]
                self.at += n
                if dt != F32:
                    v = v.bitcast(dt)
                names = "abcd"[:len(shape)]
                if len(shape) > 1:
                    v = v.rearrange("p (" + " ".join(names) + ") -> p " + " ".join(names),
                                    **{k: s for k, s in zip(names, shape)})
                return v

            def pair(self, shape):
                return self.take(shape, F16), self.take(shape, F16)

        lay = Layout()
        stage = lay.take([2, EW * 2])
        est = [lay.pair([2 * EW]) for _ in range(2)]
        tstage = [lay.take([DC * HID]) for _ in range(2)]
        lay = Layout()
        ctx_tok = lay.take([NCTX // P, D])
        cT = lay.pair([DC, NKV])
        heads_at = lay.at
        av = lay.pair([NT + 1, D])
        lay = Layout(heads_at + 4 * NKV)
        aff = lay.take([2, S])
        aqT = lay.pair([DC, S])
        akT = tuple(t[:, :, BL:BL + S] for t in akT_pad)
        a_s = lay.take([4, 2 * P])
        a_p = lay.take([4, 2 * P])
        lat = lay.take([NT, D])
        a_pT = lay.pair([8, P])
        assert lay.at <= heads_at + 40 * 1024
        lay = Layout(heads_at)
        kT = [lay.pair([NKV]) for _ in range(2)]
        qT = [lay.pair([S]) for _ in range(2)]
        v = [lay.pair([KT_TILES, P]) for _ in range(2)]
        xp = lay.take([NKV])
        xpT = lay.pair([KT_TILES, P])
        rt_x = lay.take([S])
        on = lay.take([NT, P])
        oT = lay.pair([XH, S])
        lay = Layout()
        hp = lay.take([2, S + 2])
        conv = lay.take([2, 3, S])
        g = lay.take([NM, S])
        gt = lay.take([2, HID])
        gi = lay.take([2, HID], F16)
        gq = lay.take([NM, S], F16)
        lay = Layout()
        qs = lay.take([LH, S], F16)
        ks = lay.take([LH, NCTX], F16)
        VW = 2 * LD + 2
        v16 = lay.take([NCTX // P, LH, VW], F16)
        os_at = lay.at
        os_ = lay.take([NT, LH, VW])
        lp = lay.take([2, 1024])
        lpT = [lay.pair([8, P]) for _ in range(2)]
        crT = lay.pair([DC, NCTX])
        craw = lay.take([DC, NCTX])
        lay = Layout(os_at)
        dq = lay.pair([DC, S])
        dk = lay.pair([DC, NCTX])
        rt = lay.take([2, 2, S])
        assert lay.at <= os_at + 4 * (NT * LH * VW + 2048) + 4096
        lay = Layout()
        ew = lay.take([2, NE * EW], F16)
        hg = lay.take([2, DC, S])
        hgT = [lay.pair([DC, S]) for _ in range(2)]
        lg = lay.take([6, NT, NE])
        mT = lay.take([S], F16)

        ps = c_.enter_context(nc.psum_tensor("ps", [P, 8, 512], F32))

        def banks(k, n):
            return ps[:, k:k + n, :].rearrange("p k n -> p (k n)")

        ew_d = nc.dram_tensor("ew_d", (2, P, NE * EW), F16, kind="Internal").ap()
        qd = nc.dram_tensor("qd", (2, D, S), F16, kind="Internal").ap()
        kd = nc.dram_tensor("kd", (2, D, NCTX), F16, kind="Internal").ap()

        const_in, pads_set = sig("const_in"), sig("pads_set")
        w_in = [sig(f"w_in{i}") for i in range(2)]
        w_hi, w_lo = sig("w_hi"), sig("w_lo", 0, 1)
        ew_out = [sig(f"ew_out{i}", 0, 1) for i in range(2)]
        t_in, t_sum, t_all, t_done = sig("t_in"), sig("t_sum"), sig("t_all"), sig("t_done")
        x_in, ctx_in_s, craw_in, ew_in = (sig("x_in", 16), sig("ctx_in", 16), sig("craw_in", 16),
                                          sig("ew_in", 32))
        x_out = sig("x_out", 16, 1)
        k_out, q_out, qk_in = sig("k_out", 6 * 16), sig("q_out", 4 * 16), sig("qk_in", 15 * 16)
        var_ready, rstd_ready = sig("var_ready", 9), sig("rstd_ready", 9)
        y_ready, y_t, y_hi, y_lo = sig("y_ready", 10), sig("y_t", 20), sig("y_hi", 20), sig("y_lo", 20)
        aff_done = sig("aff_done", 6)
        a_proj, a_q, a_hi, a_lo = sig("a_proj", 7), sig("a_q", 2), sig("a_hi", 7), sig("a_lo", 7)
        a_scores, a_max, a_exp = sig("a_scores", 1), sig("a_max", 1), sig("a_exp", 1)
        a_pt, a_pthi, a_ptlo, a_out = sig("a_pt", 1), sig("a_pthi", 1), sig("a_ptlo", 1), sig("a_out", 1)
        NU = 8 * XH
        NTI = NT * XH
        u_mm, u_hi, u_lo, u_q = sig("u_mm", NU), sig("u_hi", NU), sig("u_lo", NU, 1), sig("u_q", XH)
        s_mm, s_max, s_exp = sig("s_mm", NTI), sig("s_max", NTI), sig("s_exp", NTI)
        pt_mm, pt_hi, pt_lo = sig("pt_mm", 3 * NTI), sig("pt_hi", 3 * NTI), sig("pt_lo", 3 * NTI)
        o_mm, o_done = sig("o_mm", NTI), sig("o_done", NTI, 1)
        xo_mm, xo_added = sig("xo_mm", 1), sig("xo_added", 1)
        h_mm, h_pad, h_conv, h_silu = sig("h_mm", NM), sig("h_pad", NM), sig("h_conv", NM), sig("h_silu", NM)
        g_t, g_quant, gq_t, gq_done = sig("g_t", NT), sig("g_quant", NT), sig("gq_t", NT), sig("gq_done", NT)
        f_mm, f_added = sig("f_mm", NT), sig("f_added", NT)
        lq_mm, lq_q, lq_hi, lq_lo = sig("lq_mm", 4), sig("lq_q", 2), sig("lq_hi", 4), sig("lq_lo", 4)
        rows_zero = sig("rows_zero", 2)
        cr_hi, cr_lo = sig("cr_hi", DC), sig("cr_lo", DC)
        rp_mm, rp_sum, rp_hi, rp_lo = sig("rp_mm", 6), sig("rp_sum", 6), sig("rp_hi", 6), sig("rp_lo", 6, 1)
        lv_mm, lv_hi, lv_lo = sig("lv_mm", 6), sig("lv_hi", 6), sig("lv_lo", 6)
        ones_set = sig("ones_set", 1)
        UD, UE = 32, 64
        UN = UD + UE
        ls_mm, ls_max, ls_exp = sig("ls_mm", UN), sig("ls_max", UN), sig("ls_exp", UN)
        lt_mm, lt_hi, lt_lo = sig("lt_mm", 2 * UN), sig("lt_hi", 2 * UN), sig("lt_lo", 2 * UN)
        lo_mm, lo_done = sig("lo_mm", UN), sig("lo_done", UN // 4, 1)
        lx_mm, lx_added = sig("lx_mm", 2), sig("lx_added", 2)
        r_logits, r_onehot, r_oT, r_mT, r_b2 = (sig("r_logits", 1), sig("r_onehot", 1), sig("r_oT", 1),
                                               sig("r_mT", 1), sig("r_b2", 1))
        e_h, e_gelu, e_split, e_y, e_added = (sig("e_h", 2 * NE), sig("e_gelu", 2 * NE),
                                              sig("e_split", NE, 1), sig("e_y", NE), sig("e_added", NE, 1))
        dve_own = sig("dve_own")
        passed = sig("passed")

        def W(name, c, n0, n):
            width = next(w_ for k_, _, w_ in RESIDENT if k_ == name)
            at = OFF[name] + c * width + n0
            return wh[:, bass.ds(at, n)], wl[:, bass.ds(at, n)]

        def C(name, i=0):
            return col[:, bass.ds(COL[name] + i, 1)]

        def R(name, n=D):
            return row[:, ROW[name]:ROW[name] + n]

        def both(pair, *at):
            return tuple(t[at] for t in pair)

        def rows4(v_, n=NT):
            return v_.unsqueeze(1).to_broadcast([P, n, v_.shape[-1]])

        def alone(eng):
            eng.sem_inc(passed.sem, 1)

        CTX_AT = (7, 0)
        FIRST = (0, 1, 4, 5, 2, 3, 6)
        CTX_DST = [both(cT, slice(None), slice(None), slice(512 * k, 512 * k + 512)) for k in range(3)]
        XS = float(np.float32(XD ** -0.5))
        MODES = [dict(nk=S, heads=2, bodies=8, first=0, body0=0), dict(nk=NCTX, heads=1, bodies=16, first=UD, body0=8)]

        block = c_.enter_context(nc.Block())

        @block.sync
        def _(sp):
            for signal in (x_out, *ew_out):
                sp.sem_inc(signal.sem, 1)
            consts = [(col, col_in), (row, row_in), (b2, b2_in), (mask, mask_in), (rope_q, rope_q_in),
                      (rope_k, rope_k_in), (ident, ident_in), (ident16, ident16_in)]
            for dst, src in consts:
                sp.dma_start(dst[:], src).then_inc(const_in.sem, 16)
            for k in range(2):
                sp.dma_start(tstage[k], tern_in[k]).then_inc(t_in.sem, 16)
            with sp.Fori(0, WCH // 2) as it:
                for s_ in range(2):
                    sp.wait_ge(w_lo.sem, w_lo.at(0, 2 * it))
                    alone(sp)
                    sp.dma_start(stage[:, s_, 0:WC], w_dram[:, bass.ds((2 * it + s_) * WC, WC)]).then_inc(w_in[s_].sem, 16)
            with sp.Fori(0, 2) as it:
                for s_ in range(2):
                    sp.wait_ge(w_lo.sem, w_lo.at(0, WCH + 2 * it))
                    alone(sp)
                    sp.dma_start(stage[:, s_, :], moe_in[:, bass.ds(it * 4 * EW + s_ * 2 * EW, 2 * EW)])\
                      .then_inc(w_in[s_].sem, 16)
                for s_ in range(2):
                    sp.wait_ge(w_lo.sem, w_lo.at(0, WCH + 2 * it + s_ + 1))
                    alone(sp)
                    for part in range(2):
                        sp.dma_start(ew_d[part, :, bass.ds(it * 4 * EW + s_ * 2 * EW, 2 * EW)],
                                     est[s_][part]).then_inc(ew_out[s_].sem, 16)
            sp.wait_ge(w_lo.sem, w_lo.at(0, WCH + 4))
            for s_ in range(2):
                sp.wait_ge(ew_out[s_].sem, ew_out[s_].at(0, 64))
            sp.wait_ge(t_done.sem, 2)
            with sp.Fori(0, B) as b:
                sp.wait_ge(x_out.sem, x_out.at(b, 0))
                alone(sp)
                sp.dma_start(x[:], x_dram[bass.ds(b, 1)].rearrange("b (i p) d -> p (b i) d", p=P)).then_inc(x_in.sem, 16)
                sp.wait_ge(e_added.sem, e_added.at(b, 0))
                alone(sp)
                sp.dma_start(ctx_tok, ctx_dram[bass.ds(b, 1)].rearrange("b (i p) d -> p (b i) d", p=P)).then_inc(ctx_in_s.sem, 16)
                sp.wait_ge(xo_added.sem, xo_added.at(b, 1))
                alone(sp)
                sp.dma_start(craw, ctxT_dram[bass.ds(b, 1)].rearrange("b (c p) t -> p (b c) t", p=P)).then_inc(craw_in.sem, 16)
                def send(split, d_, src, n, c0, c1, done):
                    sp.wait_ge(split[0].sem, split[0].at(b, split[1]))
                    alone(sp)
                    for part in range(2):
                        sp.dma_start(d_[part, P * c0:P * c1, 0:n].rearrange("(c p) t -> p c t", p=P),
                                     src[part][:, c0:c1, 0:n]).then_inc(done.sem, 16)

                def stack(sent, count, d_, heads, n, c0, c1):
                    sp.wait_ge(sent.sem, sent.at(b, 16 * count))
                    alone(sp)
                    sp.wait_ge(rows_zero.sem, rows_zero.at(b, 2))
                    alone(sp)
                    for r_, part in enumerate((0, 1, 0) if d_ is qd else (0, 0, 1)):
                        sp.dma_start(heads[16 * r_:16 * r_ + 16, P // LD * c0:P // LD * c1, 0:n],
                                     d_[part, P * c0:P * c1, 0:n].rearrange("(h d) t -> d h t", d=LD))\
                          .then_inc(qk_in.sem, 16)

                send((lq_lo, 2), kd, dk, S, 0, 2, k_out)
                send((lq_lo, 4), qd, dq, S, 0, 2, q_out)
                stack(k_out, 2, kd, ks, S, 0, 2)
                stack(q_out, 2, qd, qs, S, 0, 2)
                for c in range(DC):
                    send((rp_lo, 2 * c + 2), kd, dk, NCTX, c, c + 1, k_out)
                    sp.wait_ge(ls_mm.sem, ls_mm.at(b, UD))
                    alone(sp)
                    stack(k_out, 4 + 2 * c, kd, ks, NCTX, c, c + 1)
                send((rp_lo, 6), qd, dq, S, 0, 2, q_out)
                stack(q_out, 4, qd, qs, S, 0, 2)
                sp.wait_ge(ls_mm.sem, ls_mm.at(b, UN))
                for part in range(2):
                    sp.dma_start(ew[:, part, :], ew_d[part]).then_inc(ew_in.sem, 16)
                sp.wait_ge(e_added.sem, e_added.at(b, NE))
                alone(sp)
                sp.dma_start(out[bass.ds(b, 1)].rearrange("b (i p) d -> p (b i) d", p=P), x[:]).then_inc(x_out.sem, 16)
            sp.wait_ge(x_out.sem, x_out.at(B, 0))

        @block.gpsimd
        def _(pool):
            def zero_rows(t):
                nc.gpsimd.memset(t[0:KR].rearrange("p h t -> p (h t)").bitcast(F32), 0.0).then_inc(rows_zero.sem, 1)

            nc.gpsimd.memset(ones[:], 1.0).then_inc(pads_set.sem, 1)
            for t in (*y_pad, *akT_pad):
                nc.gpsimd.memset(t[:, :, 0:BL], 0.0).then_inc(pads_set.sem, 1)
                nc.gpsimd.memset(t[:, :, BL + S:], 0.0).then_inc(pads_set.sem, 1)
            pool.wait_ge(const_in.sem, 16 * 8)
            with pool.Fori(0, B) as b:
                for k in range(9):
                    if k == 6:
                        pool.wait_ge(h_silu.sem, h_silu.at(b, NM))
                        alone(pool)
                        zero_rows(qs)
                    pool.wait_ge(var_ready.sem, var_ready.at(b, k + 1))
                    nc.gpsimd.tensor_tensor(rstd[:], ve[:], col[:, COL["half"]:COL["half"] + NT], ALU.pow)\
                      .then_inc(rstd_ready.sem, 1)
                    if k == 6:
                        zero_rows(ks)

        @block.tensor
        def _(pe):
            mm = nc.tensor.matmul

            def product(out_, pairs):
                last, n = None, len(pairs)
                for k, ((lh, ll), (rh, rl_)) in enumerate(pairs):
                    mm(out_, lh, rh, start=(k == 0), stop=False)
                    mm(out_, lh, rl_, start=False, stop=False)
                    last = mm(out_, ll, rh, start=False, stop=(k == n - 1))
                return last

            def transpose_y(b, k, at=(0, 1)):
                pe.wait_ge(y_ready.sem, y_ready.at(b, k + 1))
                for c in range(DC):
                    for i in range(NT):
                        last = nc.tensor.transpose(ps[:, at[c], P * i:P * i + P], y[:, i, P * c:P * c + P], ident[:])
                    last.then_inc(y_t.sem, 1)

            pe.wait_ge(pads_set.sem, 9)
            pe.wait_ge(t_sum.sem, 2)
            mm(ps[:, 0, 0:2], ones[:], wsum[:], start=True, stop=True).then_inc(t_all.sem, 1)
            pe.wait_ge(t_done.sem, 2)
            pe.wait_ge(w_lo.sem, w_lo.at(0, WCH + 4))
            pe.wait_ge(const_in.sem, 16 * 8)

            def windowed(b):
                transpose_y(b, 0)
                pe.wait_ge(y_lo.sem, y_lo.at(b, 2))
                for j, (name, m) in enumerate([("aq", 0), ("aq", 1), ("ak", 0), ("ak", 1)]):
                    product(ps[:, 2 + j, :], [(W(name, c, P * m, P), both(yT, slice(None), c)) for c in range(DC)])\
                        .then_inc(a_proj.sem, 1)
                for j in range(NT + 1):
                    last = product(ps[:, (6, 6, 7, 7, 0)[j], D * (j % 2):D * (j % 2) + D],
                                   [(both(y_pad, slice(None), c, slice(P * j, P * j + P)), W("av", c, 0, D))
                                    for c in range(DC)])
                    if j % 2 or j == NT:
                        last.then_inc(a_proj.sem, 1)
                pe.wait_ge(a_lo.sem, a_lo.at(b, 4))
                for p_ in range(4):
                    last = product(ps[:, 1 + p_ // 2, 256 * (p_ % 2):256 * (p_ % 2) + 256],
                                   [(both(aqT, slice(None), c, slice(P * p_, P * p_ + P)),
                                     both(akT_pad, slice(None), c, slice(P * p_, P * p_ + 2 * P))) for c in range(DC)])
                last.then_inc(a_scores.sem, 1)
                pe.wait_ge(a_lo.sem, a_lo.at(b, 7))
                transpose_y(b, 1, CTX_AT)
                pe.wait_ge(a_exp.sem, a_exp.at(b, 1))
                for n in range(8):
                    last = nc.tensor.transpose(ps[:, 3 + n // 4, P * (n % 4):P * (n % 4) + P],
                                               a_p[:, n // 2, P * (n % 2):P * (n % 2) + P], ident[:])
                last.then_inc(a_pt.sem, 1)
                pe.wait_ge(a_ptlo.sem, a_ptlo.at(b, 1))
                for p_ in range(4):
                    last = product(ps[:, 5 + p_ // 2, 256 * (p_ % 2):256 * (p_ % 2) + 256],
                                   [(both(a_pT, slice(None), 2 * p_ + kc), both(av, slice(None), p_ + kc))
                                    for kc in range(2)])
                last.then_inc(a_out.sem, 1)
                transpose_y(b, 2, CTX_AT)

            def unit(b, h, par, k, n):
                pe.wait_ge(u_lo.sem, u_lo.at(b, n))
                if k < 3:
                    last = product(ps[:, 7, :], [(W("xkv", c, h * XD, XD), both(cT, slice(None), c, slice(512 * k, 512 * k + 512)))
                                                 for c in range(DC)])
                elif k == 3:
                    last = product(ps[:, 7, :], [(W("xq", c, h * XD, XD), both(cT, slice(None), c, slice(NCTX, NKV)))
                                                 for c in range(DC)])
                else:
                    for t in range(4):
                        a0 = P * (4 * (k - 4) + t)
                        last = product(ps[:, 7, P * t:P * t + P],
                                       [(both(cT, slice(None), c, slice(a0, a0 + P)), W("xkv", c, h * XD + XIN, XD))
                                        for c in range(DC)])
                last.then_inc(u_mm.sem, 1)

            def scores(b, par, i):
                for t in range(3):
                    last = product(ps[:, t, :], [(both(qT[par], slice(None), slice(P * i, P * i + P)),
                                                  both(kT[par], slice(None), slice(512 * t, 512 * t + 512)))])
                last.then_inc(s_mm.sem, 1)

            def head(b, h, par, last_head):
                for i in range(NT):
                    n = h * NT + i
                    pe.wait_ge(s_exp.sem, s_exp.at(b, n + 1))
                    for g_ in range(3):
                        for t in range(4):
                            kt = 4 * g_ + t
                            last = nc.tensor.transpose(ps[:, 3 + g_, P * t:P * t + P], xp[:, P * kt:P * kt + P], ident[:])
                        last.then_inc(pt_mm.sem, 1)
                    if i < NT - 1:
                        scores(b, par, i + 1)
                    elif not last_head:
                        pe.wait_ge(u_lo.sem, u_lo.at(b, 7 + 8 * h + 4))
                        scores(b, 1 - par, 0)
                    k = 2 * i
                    if not last_head:
                        unit(b, h + 1, 1 - par, k, 7 + 8 * h + k)
                    pe.wait_ge(pt_lo.sem, pt_lo.at(b, 3 * (n + 1)))
                    pe.wait_ge(o_done.sem, o_done.at(b, n))
                    if i == 0:
                        pe.wait_ge(u_lo.sem, u_lo.at(b, 7 + 8 * h - 0) if not last_head else u_lo.at(b, 7 + 8 * h))
                    product(ps[:, 6, P * i:P * i + P],
                            [(both(xpT, slice(None), kt), both(v[par], slice(None), kt)) for kt in range(KT_TILES)])\
                        .then_inc(o_mm.sem, 1)
                    k = 2 * i + 1
                    if k < 7:
                        if not last_head:
                            unit(b, h + 1, 1 - par, k, 7 + 8 * h + k)
                    else:
                        before = 7 + 8 * h + (0 if last_head else 7)
                        pe.wait_ge(u_lo.sem, u_lo.at(b, before))
                        pe.wait_ge(o_done.sem, o_done.at(b, n + 1))
                        for t in range(NT):
                            last = nc.tensor.transpose(ps[:, 7, P * t:P * t + P], on[:, t, :], ident[:])
                        last.then_inc(u_mm.sem, 1)

            def latent(b):
                pe.wait_ge(y_lo.sem, y_lo.at(b, 6))
                for n in range(2):
                    unit(b, 0, 0, FIRST[n], n)
                transpose_y(b, 3)
                for n in range(2, 7):
                    if n == 4:
                        pe.wait_ge(y_lo.sem, y_lo.at(b, 8))
                    unit(b, 0, 0, FIRST[n], n)
                pe.wait_ge(u_lo.sem, u_lo.at(b, 6))
                scores(b, 0, 0)
                with pe.Fori(0, XH // 2 - 1) as hp_:
                    for s_ in range(2):
                        head(b, 2 * hp_ + s_, s_, False)
                head(b, XH - 2, 0, False)
                head(b, XH - 1, 1, True)
                pe.wait_ge(u_lo.sem, u_lo.at(b, NU))
                for i in range(NT):
                    last = product(ps[:, i // 2, D * (i % 2):D * (i % 2) + D],
                                   [(both(oT, slice(None), h, slice(P * i, P * i + P)), W("xo", h, 0, D))
                                    for h in range(XH)])
                last.then_inc(xo_mm.sem, 1)

            def bitnet(b):
                transpose_y(b, 4)
                pe.wait_ge(y_lo.sem, y_lo.at(b, 10))
                for m in range(NM):
                    if m >= 2:
                        pe.wait_ge(h_pad.sem, h_pad.at(b, m - 1))
                    for c in range(DC):
                        for part in range(2):
                            last = mm(ps[:, 2 + m % 2, :], tern[:, 0, HID * c + P * m:HID * c + P * m + P],
                                      yT[part][:, c, :], start=(c + part == 0), stop=(c + part == 2))
                    last.then_inc(h_mm.sem, 1)
                pe.wait_ge(h_silu.sem, h_silu.at(b, NM))
                for i in range(NT + 1):
                    if i < NT:
                        if i >= 2:
                            pe.wait_ge(g_quant.sem, g_quant.at(b, i - 1))
                        for m in range(NM):
                            last = nc.tensor.transpose(ps[:, 4 + 2 * (i % 2) + m // 4, P * (m % 4):P * (m % 4) + P],
                                                       g[:, m, P * i:P * i + P], ident[:])
                        last.then_inc(g_t.sem, 1)
                    if i >= 1:
                        j = i - 1
                        pe.wait_ge(g_quant.sem, g_quant.at(b, j + 1))
                        if j >= 2:
                            pe.wait_ge(gq_done.sem, gq_done.at(b, j - 1))
                        dst = ps[:, j % 2, :].bitcast(F16)
                        for m in range(NM):
                            last = nc.tensor.transpose(dst[:, P * m:P * m + P], gi[:, j % 2, P * m:P * m + P], ident16[:])
                        last.then_inc(gq_t.sem, 1)
                        pe.wait_ge(gq_done.sem, gq_done.at(b, j + 1))
                        if j >= 2:
                            pe.wait_ge(f_added.sem, f_added.at(b, j - 1))
                        for m in range(NM):
                            last = mm(ps[:, 2 + j % 2, 0:D], gq[:, m, P * j:P * j + P], tern[:, 1, D * m:D * m + D],
                                      start=(m == 0), stop=(m == NM - 1))
                        last.then_inc(f_mm.sem, 1)

            def unit_scores(b, mode, it, k, ahead=0):
                kk = k + ahead
                it, kk = it + kk // 4, kk % 4
                u = mode["first"] + it * 4 + kk
                if not (isinstance(it, int) and it == 0 and kk < 2):
                    pe.wait_ge(ls_exp.sem, ls_exp.at(b, u - 1))
                for t in range(2):
                    if mode["heads"] == 2:
                        h, i, k0 = 2 * it + kk // 2, 2 * (kk % 2) + t, 0
                    else:
                        h, i, k0 = it, kk, 512 * t
                    last = mm(ps[:, 2 * (kk % 2) + t, :], qs[0:KR, bass.ds(h, 1), P * i:P * i + P].rearrange("p a n -> p (a n)"),
                              ks[0:KR, bass.ds(h, 1), k0:k0 + 512].rearrange("p a n -> p (a n)"), start=True, stop=True)
                last.then_inc(ls_mm.sem, 1)

            def unit_transpose(b, mode, it, k, ahead=0):
                kk = k + ahead
                it, kk = it + kk // 4, kk % 4
                u = mode["first"] + it * 4 + kk
                pe.wait_ge(ls_exp.sem, ls_exp.at(b, u + 1))
                for g_ in range(2):
                    if not (isinstance(it, int) and it + kk == 0):
                        pe.wait_ge(lt_lo.sem, lt_lo.at(b, 2 * u - 1 + g_))
                    for t in range(4):
                        n = 4 * g_ + t
                        last = nc.tensor.transpose(ps[:, 4 + g_, P * t:P * t + P], lp[:, kk % 2, P * n:P * n + P], ident[:])
                    last.then_inc(lt_mm.sem, 1)

            def unit_out(b, mode, it, k):
                u = mode["first"] + it * 4 + k
                pe.wait_ge(lt_lo.sem, lt_lo.at(b, 2 * (u + 1)))
                if k == 0:
                    pe.wait_ge(lo_done.sem, lo_done.at(b, mode["body0"] + it))
                two = mode["heads"] == 2
                nkt = mode["nk"] // P
                for t in range(2 if two else 1):
                    i = 2 * (k % 2) + t if two else k
                    h = 2 * it + k // 2 if two else it
                    o0 = (i * 2 + k // 2) * VW if two else i * VW
                    for kt in range(nkt):
                        n = t * nkt + kt
                        hi, lo = (part[:, n, :] for part in lpT[k % 2])
                        mm(ps[:, 6, o0:o0 + VW - 1], hi,
                           v16[:, kt, bass.ds(h, 1), 0:VW - 1].rearrange("p a n -> p (a n)"), start=(kt == 0), stop=False)
                        last = mm(ps[:, 6, o0:o0 + 1 + LD], lo,
                                  v16[:, kt, bass.ds(h, 1), 0:1 + LD].rearrange("p a n -> p (a n)"), start=False, stop=(kt == nkt - 1))
                last.then_inc(lo_mm.sem, 1)

            def attend(b, m_):
                mode = MODES[m_]
                pe.wait_ge(lv_lo.sem, lv_lo.at(b, (2, 6)[m_]))
                pe.wait_ge(qk_in.sem, qk_in.at(b, (96, 240)[m_]))
                for u in range(3):
                    unit_scores(b, mode, 0, u)
                nb = mode["bodies"]
                unit_transpose(b, mode, 0, 0)
                unit_scores(b, mode, 0, 3)
                with pe.Fori(0, nb - 1) as it:
                    for k in range(4):
                        unit_transpose(b, mode, it, k, 1)
                        unit_scores(b, mode, it, k, 4)
                        unit_out(b, mode, it, k)
                for k in range(4):
                    if k < 3:
                        unit_transpose(b, mode, nb - 1, k, 1)
                    unit_out(b, mode, nb - 1, k)
                transpose_y(b, 6 + 2 * m_)
                pe.wait_ge(y_lo.sem, y_lo.at(b, 2 * (7 + 2 * m_)))
                for i in range(NT):
                    last = product(ps[:, 2 + i // 2, D * (i % 2):D * (i % 2) + D],
                                   [(both(yT, slice(None), c, slice(P * i, P * i + P)), W(("so", "co")[m_], c, 0, D))
                                    for c in range(DC)])
                last.then_inc(lx_mm.sem, 1)

            def self_attention(b):
                transpose_y(b, 5)
                pe.wait_ge(y_lo.sem, y_lo.at(b, 12))
                for j, (name, m) in enumerate([("sk", 0), ("sk", 1), ("sq", 0), ("sq", 1)]):
                    product(ps[:, 2 + j, :], [(W(name, c, P * m, P), both(yT, slice(None), c)) for c in range(DC)])\
                        .then_inc(lq_mm.sem, 1)
                for i in range(NT):
                    last = product(ps[:, 6 + i // 2, D * (i % 2):D * (i % 2) + D],
                                   [(both(yT, slice(None), c, slice(P * i, P * i + P)), W("sv", c, 0, D)) for c in range(DC)])
                    if i % 2:
                        last.then_inc(lv_mm.sem, 1)
                attend(b, 0)

            def cross_attention(b):
                pe.wait_ge(cr_lo.sem, cr_lo.at(b, DC))
                for j in range(6):
                    if j == 2:
                        transpose_y(b, 7)
                    if j == 4:
                        pe.wait_ge(y_lo.sem, y_lo.at(b, 16))
                    if j >= 2:
                        pe.wait_ge(rp_sum.sem, rp_sum.at(b, j - 1))
                    m = j - 4 if j >= 4 else j // 2
                    t0 = 512 * (j % 2)
                    src = [both(yT, slice(None), c) if j >= 4 else both(crT, slice(None), c, slice(t0, t0 + 512)) for c in range(DC)]
                    for s_, name in enumerate((("cq", "cqs") if j >= 4 else ("ck", "cks"))):
                        last = product(ps[:, 4 + 2 * (j % 2) + s_, :], [(W(name, c, P * m, P), src[c]) for c in range(DC)])
                    last.then_inc(rp_mm.sem, 1)
                pe.wait_ge(lx_added.sem, lx_added.at(b, 1))
                for i in range(NCTX // P):
                    if i % 2 == 0 and i >= 4:
                        pe.wait_ge(lv_lo.sem, lv_lo.at(b, i // 2 + 1))
                    last = product(ps[:, 2 + (i // 2) % 2, D * (i % 2):D * (i % 2) + D],
                                   [(both(crT, slice(None), c, slice(P * i, P * i + P)), W("cv", c, 0, D)) for c in range(DC)])
                    if i % 2:
                        last.then_inc(lv_mm.sem, 1)
                attend(b, 1)

            def expert_hidden(b, e, par):
                for m in range(DC):
                    last = product(ps[:, 2 * par + m, :],
                                   [(tuple(ew[:, part, bass.ds(e * EW + D * c + P * m, P)] for part in range(2)),
                                     both(yT, slice(None), c)) for c in range(DC)])
                    last.then_inc(e_h.sem, 1)

            def expert_out(b, e, par):
                pe.wait_ge(e_split.sem, e_split.at(b, e + 1))
                for i in range(NT):
                    last = product(ps[:, 4 + 2 * par + i // 2, D * (i % 2):D * (i % 2) + D],
                                   [(both(hgT[par], slice(None), c, slice(P * i, P * i + P)),
                                     tuple(ew[:, part, bass.ds(e * EW + DC * D + D * c, D)] for part in range(2)))
                                    for c in range(DC)])
                last.then_inc(e_y.sem, 1)

            def routed(b):
                transpose_y(b, 9)
                pe.wait_ge(y_lo.sem, y_lo.at(b, 20))
                for i in range(NT):
                    last = product(ps[:, 2, NE * i:NE * i + NE],
                                   [(both(yT, slice(None), c, slice(P * i, P * i + P)), W("g", c, 0, NE)) for c in range(DC)])
                last.then_inc(r_logits.sem, 1)
                pe.wait_ge(ew_in.sem, ew_in.at(b, 32))
                expert_hidden(b, 0, 0)
                pe.wait_ge(r_onehot.sem, r_onehot.at(b, 1))
                oh = lg[:, 5, :, :].bitcast(F16)
                for i in range(NT):
                    last = mm(ps[0:NE, 3, P * i:P * i + P], oh[:, i, 0:NE], ident16[:], start=True, stop=True)
                last.then_inc(r_oT.sem, 1)
                pe.wait_ge(r_mT.sem, r_mT.at(b, 1))
                for i in range(NT):
                    d_ = ps[:, 4 + i // 2, D * (i % 2):D * (i % 2) + D]
                    mm(d_, mT[0:NE, P * i:P * i + P], b2h[:], start=True, stop=False)
                    last = mm(d_, mT[0:NE, P * i:P * i + P], b2l[:], start=False, stop=True)
                last.then_inc(r_b2.sem, 1)
                with pe.Fori(0, NE // 2 - 1) as it:
                    for s_ in range(2):
                        expert_hidden(b, 2 * it + s_ + 1, 1 - s_)
                        expert_out(b, 2 * it + s_, s_)
                expert_hidden(b, NE - 1, 1)
                expert_out(b, NE - 2, 0)
                expert_out(b, NE - 1, 1)

            with pe.Fori(0, B) as b:
                windowed(b)
                latent(b)
                bitnet(b)
                self_attention(b)
                cross_attention(b)
                routed(b)

        @block.scalar
        def _(act):
            A = nc.scalar.activation
            act.sem_inc(lo_done.sem, 1)

            with act.Fori(0, WCH // 2) as it:
                for s_ in range(2):
                    act.wait_ge(w_in[s_].sem, 16 * it + 16)
                    A(wh[:, bass.ds((2 * it + s_) * WC, WC)], stage[:, s_, 0:WC], ACT.Copy).then_inc(w_hi.sem, 1)
            with act.Fori(0, 2) as it:
                for s_ in range(2):
                    act.wait_ge(w_in[s_].sem, 16 * (WCH // 2) + 16 * it + 16)
                    act.wait_ge(ew_out[s_].sem, ew_out[s_].at(0, 32 * it))
                    A(est[s_][0], stage[:, s_, :], ACT.Copy).then_inc(w_hi.sem, 1)
            act.wait_ge(const_in.sem, 16 * 8)
            A(b2h[:], b2[:], ACT.Copy).then_inc(w_hi.sem, 1)

            def split_hi(b, k, dst, bias=None, aff_k=None):
                for c in range(DC):
                    if aff_k is not None:
                        act.wait_ge(aff_done.sem, aff_done.at(b, 2 * aff_k + c + 1))
                        A(dst[0][:, c, :], aff[:, c, :], ACT.Copy).then_inc(y_hi.sem, 1)
                        continue
                    act.wait_ge(y_t.sem, y_t.at(b, 2 * k + c + 1))
                    if bias:
                        A(dst[0][:, c, :], ps[:, c, :], ACT.Identity, bias=C(bias, c)).then_inc(y_hi.sem, 1)
                    else:
                        A(dst[0][:, c, :], ps[:, c, :], ACT.Copy).then_inc(y_hi.sem, 1)

            def windowed(b):
                split_hi(b, 0, yT)
                for j in range(7):
                    if j < 2:
                        act.wait_ge(a_q.sem, a_q.at(b, j + 1))
                        A(aqT[0][:, j, :], aff[:, j, :], ACT.Copy).then_inc(a_hi.sem, 1)
                        continue
                    act.wait_ge(a_proj.sem, a_proj.at(b, j + 1))
                    if j < 4:
                        A(akT[0][:, j - 2, :], ps[:, 2 + j, :], ACT.Identity, bias=C("abk", j - 2)).then_inc(a_hi.sem, 1)
                    elif j < 6:
                        A(av[0][:, 2 * (j - 4):2 * (j - 4) + 2, :].rearrange("p a n -> p (a n)"), ps[:, 2 + j, :], ACT.Copy)\
                            .then_inc(a_hi.sem, 1)
                    else:
                        A(av[0][:, NT, :], ps[:, 0, 0:D], ACT.Copy).then_inc(a_hi.sem, 1)
                act.wait_ge(a_max.sem, a_max.at(b, 1))
                for p_ in range(4):
                    last = A(a_p[:, p_, :], a_s[:, p_, :], ACT.Exp, bias=nm[:, p_:p_ + 1], accum_out=sums[:, p_:p_ + 1])
                last.then_inc(a_exp.sem, 1)
                split_hi(b, 1, CTX_DST[0], aff_k=0)
                act.wait_ge(a_pt.sem, a_pt.at(b, 1))
                A(a_pT[0].rearrange("p a n -> p (a n)"), banks(3, 2), ACT.Copy).then_inc(a_pthi.sem, 1)

            def unit_hi(b, h, par, k, n):
                if k == 3:
                    act.wait_ge(u_q.sem, u_q.at(b, h + 1))
                    A(qT[par][0], rt_x, ACT.Copy).then_inc(u_hi.sem, 1)
                    return
                act.wait_ge(u_mm.sem, u_mm.at(b, n + 1))
                alone(act)
                if k < 3:
                    A(kT[par][0][:, 512 * k:512 * k + 512], ps[:, 7, :], ACT.Identity, bias=C("xbk", h)).then_inc(u_hi.sem, 1)
                elif k < 7:
                    A(v[par][0][:, 4 * (k - 4):4 * (k - 4) + 4, :].rearrange("p a n -> p (a n)"), ps[:, 7, :], ACT.Copy)\
                        .then_inc(u_hi.sem, 1)
                else:
                    A(oT[0][:, bass.ds(h, 1), :].rearrange("p a n -> p (a n)"), ps[:, 7, :], ACT.Identity,
                      bias=C("xbv", h)).then_inc(u_hi.sem, 1)

            def exps(b, n, i):
                act.wait_ge(s_max.sem, s_max.at(b, n + 1))
                A(xp, banks(0, 3), ACT.Exp, bias=nm[:, i:i + 1], accum_out=sums[:, i:i + 1]).then_inc(s_exp.sem, 1)

            def head(b, h, par, last_head):
                for i in range(NT):
                    n = h * NT + i
                    for g_ in range(3):
                        act.wait_ge(pt_mm.sem, pt_mm.at(b, 3 * n + g_ + 1))
                        A(xpT[0][:, 4 * g_:4 * g_ + 4, :].rearrange("p a n -> p (a n)"), ps[:, 3 + g_, :], ACT.Copy)\
                            .then_inc(pt_hi.sem, 1)
                    if not last_head:
                        unit_hi(b, h + 1, 1 - par, 2 * i, 7 + 8 * h + 2 * i)
                    if i < NT - 1 or not last_head:
                        exps(b, n + 1, (i + 1) % NT)
                    if i == NT - 1:
                        unit_hi(b, h, par, 7, 7 + 8 * h + (0 if last_head else 7))
                    elif not last_head:
                        unit_hi(b, h + 1, 1 - par, 2 * i + 1, 7 + 8 * h + 2 * i + 1)

            def latent(b):
                split_hi(b, 2, CTX_DST[1], aff_k=1)
                for n in range(2):
                    unit_hi(b, 0, 0, FIRST[n], n)
                split_hi(b, 3, CTX_DST[2], aff_k=2)
                for n in range(2, 7):
                    unit_hi(b, 0, 0, FIRST[n], n)
                exps(b, 0, 0)
                with act.Fori(0, XH // 2 - 1) as hp_:
                    for s_ in range(2):
                        head(b, 2 * hp_ + s_, s_, False)
                head(b, XH - 2, 0, False)
                head(b, XH - 1, 1, True)

            def bitnet(b):
                split_hi(b, 4, yT)

                def silu(m):
                    act.wait_ge(h_conv.sem, h_conv.at(b, m + 1))
                    A(g[:, m, :], conv[:, m % 2, 2, :], ACT.Silu).then_inc(h_silu.sem, 1)

                for m in range(NM):
                    act.wait_ge(h_mm.sem, h_mm.at(b, m + 1))
                    if m >= 2:
                        act.wait_ge(h_conv.sem, h_conv.at(b, m - 1))
                    A(hp[:, m % 2, 1:1 + S], ps[:, 2 + m % 2, :], ACT.Copy, scale=mw[:, 0:1]).then_inc(h_pad.sem, 1)
                    if m >= 1:
                        silu(m - 1)
                silu(NM - 1)
                for j in range(NT):
                    act.wait_ge(gq_t.sem, gq_t.at(b, j + 1))
                    A(gq[:, :, P * j:P * j + P], ps[:, j % 2, :].bitcast(F16).rearrange("p (m n) -> p m n", m=NM), ACT.Copy)\
                        .then_inc(gq_done.sem, 1)

            def values_hi(b, n, t, bank=6):
                act.wait_ge(lv_mm.sem, lv_mm.at(b, n + 1))
                A(v16[:, 2 * t:2 * t + 2, :, 1:1 + LD], ps[:, bank + t % 2, :].rearrange("p (t h d) -> p t h d", t=2, d=LD), ACT.Copy)\
                    .then_inc(lv_hi.sem, 1)

            def unit_exp(b, mode, it, k, ahead=0):
                kk = k + ahead
                it, kk = it + kk // 4, kk % 4
                u = mode["first"] + it * 4 + kk
                act.wait_ge(ls_max.sem, ls_max.at(b, u + 1))
                if mode["heads"] == 2:
                    for t in range(2):
                        last = A(lp[:, kk % 2, 512 * t:512 * t + 512], ps[:, 2 * (kk % 2) + t, :], ACT.Exp,
                                 bias=nm[:, 2 * kk + t:2 * kk + t + 1])
                else:
                    last = A(lp[:, kk % 2, :], banks(2 * (kk % 2), 2), ACT.Exp, bias=nm[:, 2 * kk:2 * kk + 1])
                last.then_inc(ls_exp.sem, 1)

            def unit_hi_l(b, mode, it, k, more):
                u = mode["first"] + it * 4 + k
                if more:
                    unit_exp(b, mode, it, k, 1)
                for g_ in range(2):
                    act.wait_ge(lt_mm.sem, lt_mm.at(b, 2 * u + g_ + 1))
                    A(lpT[k % 2][0][:, 4 * g_:4 * g_ + 4, :].rearrange("p a n -> p (a n)"), ps[:, 4 + g_, :], ACT.Copy)\
                        .then_inc(lt_hi.sem, 1)

            def body_out(b, mode, it):
                act.wait_ge(lo_mm.sem, lo_mm.at(b, mode["first"] + it * 4 + 4))
                alone(act)
                hb = mode["heads"]
                src = ps[:, 6, 0:NT * hb * VW].rearrange("p (t h n) -> p t h n", t=NT, h=hb)
                A(os_[:, :, bass.ds(it * hb, hb), 0:VW - 1], src[:, :, :, 0:VW - 1], ACT.Copy).then_inc(lo_done.sem, 1)

            def attend(b, m_):
                mode = MODES[m_]
                nb = mode["bodies"]
                unit_exp(b, mode, 0, 0)
                for k in range(4):
                    unit_hi_l(b, mode, 0, k, True)
                with act.Fori(1, nb - 1) as it:
                    for k in range(4):
                        unit_hi_l(b, mode, it, k, True)
                        if k == 0:
                            body_out(b, mode, it - 1)
                for k in range(4):
                    unit_hi_l(b, mode, nb - 1, k, k < 3)
                    if k == 0:
                        body_out(b, mode, nb - 2)
                body_out(b, mode, nb - 1)
                split_hi(b, 6 + 2 * m_, yT, bias=("sbv", "cbv")[m_])

            def self_attention(b):
                split_hi(b, 5, yT)
                for j in range(4):
                    if j < 2:
                        act.wait_ge(lq_mm.sem, lq_mm.at(b, j + 1))
                        A(dk[0][:, j, 0:S], ps[:, 2 + j, :], ACT.Identity, bias=C("sbk", j)).then_inc(lq_hi.sem, 1)
                    else:
                        act.wait_ge(lq_q.sem, lq_q.at(b, j - 1))
                        A(dq[0][:, j - 2, :], rt[:, 0, j - 2, :], ACT.Copy).then_inc(lq_hi.sem, 1)
                act.wait_ge(ones_set.sem, ones_set.at(b, 1))
                for t in range(2):
                    values_hi(b, t, t)
                act.wait_ge(craw_in.sem, craw_in.at(b, 16))
                for c in range(DC):
                    A(crT[0][:, c, :], craw[:, c, :], ACT.Copy).then_inc(cr_hi.sem, 1)
                attend(b, 0)

            def cross_attention(b):
                for j in range(6):
                    if j == 1:
                        split_hi(b, 7, yT)
                    act.wait_ge(rp_sum.sem, rp_sum.at(b, j + 1))
                    t0 = 512 * (j % 2)
                    dst = dq[0][:, j - 4, :] if j >= 4 else dk[0][:, j // 2, t0:t0 + 512]
                    A(dst, rt[:, j % 2, 0, :], ACT.Copy).then_inc(rp_hi.sem, 1)
                for t in range(4):
                    values_hi(b, 2 + t, t, 2)
                attend(b, 1)

            def routed(b):
                split_hi(b, 9, yT)
                act.wait_ge(r_oT.sem, r_oT.at(b, 1))
                A(mT[0:NE, :], ps[0:NE, 3, :], ACT.Copy).then_inc(r_mT.sem, 1)
                with act.Fori(0, NE // 2) as it:
                    for s_ in range(2):
                        act.wait_ge(e_split.sem, e_split.at(b, 2 * it))
                        for m in range(DC):
                            act.wait_ge(e_h.sem, e_h.at(b, 4 * it + 2 * s_ + m + 1))
                            alone(act)
                            A(hg[:, s_, m, :], ps[:, 2 * s_ + m, :], ACT.Gelu,
                              bias=C("b1", (2 * it + s_) * DC + m)).then_inc(e_gelu.sem, 1)

            with act.Fori(0, B) as b:
                windowed(b)
                latent(b)
                bitnet(b)
                self_attention(b)
                cross_attention(b)
                routed(b)

        @block.vector
        def _(dve):
            V = nc.vector
            own = Order(dve, dve_own.sem)
            TT, TS_, STT = V.tensor_tensor, V.tensor_scalar, V.scalar_tensor_tensor

            for signal in (w_lo, u_lo, o_done, e_added, e_split, rp_lo):
                dve.sem_inc(signal.sem, 1)
            for k in range(2):
                dve.wait_ge(t_in.sem, 32)
                V.tensor_reduce(wsum[:, k:k + 1], tstage[k], AX.X, ALU.add, apply_absolute_value=True).then_inc(t_sum.sem, 1)
            with dve.Fori(0, WCH // 2) as it:
                for s_ in range(2):
                    dve.wait_ge(w_hi.sem, 2 * it + s_ + 1)
                    at = bass.ds((2 * it + s_) * WC, WC)
                    TT(wl[:, at], stage[:, s_, 0:WC], wh[:, at], ALU.subtract).then_inc(w_lo.sem, 1)
            with dve.Fori(0, 2) as it:
                for s_ in range(2):
                    dve.wait_ge(w_hi.sem, WCH + 2 * it + s_ + 1)
                    TT(est[s_][1], stage[:, s_, :], est[s_][0], ALU.subtract).then_inc(w_lo.sem, 1)
            dve.wait_ge(t_all.sem, 1)
            own.link(TS_(mw[:], ps[:, 0, 0:2], 1.0 / (D * HID), 1e-5, ALU.mult, ALU.max))
            own.link(V.reciprocal(msc[:], mw[:]))
            for k in range(2):
                own.link(TS_(tstage[k], tstage[k], msc[:, k:k + 1], ROUND, ALU.mult, ALU.add))
                own.link(TS_(tstage[k], tstage[k], ROUND, -1.0, ALU.subtract, ALU.max))
                TS_(tern[:, k, :], tstage[k], 1.0, None, ALU.min).then_inc(t_done.sem, 1)
            dve.wait_ge(w_hi.sem, WCH + 5)
            own.link(TT(b2l[:], b2[:], b2h[:], ALU.subtract))
            dve.wait_ge(const_in.sem, 16 * 8)

            def moments(b, k, src):
                for i in range(NT):
                    own.mark(V.bn_stats(st[:, i, :], src[:, i, :]))
                own.wait()
                alone(dve)
                for i in range(NT):
                    own.mark(V.bn_aggr(mv[:, i, :], st[:, i, :]))
                own.wait()
                TS_(ve[:], mv[:, :, 1], 1e-5, None, ALU.add).then_inc(var_ready.sem, 1)

            def normalise(b, k, src, dst):
                dve.wait_ge(rstd_ready.sem, rstd_ready.at(b, k + 1))
                for i in range(NT):
                    last = TS_(dst[:, i, :], src[:, i, :], mv[:, i, 0:1], rstd[:, i:i + 1], ALU.subtract, ALU.mult)
                return last

            def norm(b, k, src, dst):
                moments(b, k, src)
                return normalise(b, k, src, dst)

            def affine(b, k, aff_k, at=(0, 1)):
                gn, bn = (("gm", "bm"), ("gm", "bm"), ("gl", "bl"))[aff_k]
                for c in range(DC):
                    dve.wait_ge(y_t.sem, y_t.at(b, 2 * k + c + 1))
                    TS_(aff[:, c, :], ps[:, at[c], :], C(gn, c), C(bn, c), ALU.mult, ALU.add).then_inc(aff_done.sem, 1)

            def split_lo(b, k, dst, bias=None, aff_k=None):
                for c in range(DC):
                    dve.wait_ge(y_hi.sem, y_hi.at(b, 2 * k + c + 1))
                    if aff_k is not None:
                        ins = TT(dst[1][:, c, :], aff[:, c, :], dst[0][:, c, :], ALU.subtract)
                    elif bias:
                        ins = STT(dst[1][:, c, :], ps[:, c, :], C(bias, c), dst[0][:, c, :], ALU.add, ALU.subtract)
                    else:
                        ins = TT(dst[1][:, c, :], ps[:, c, :], dst[0][:, c, :], ALU.subtract)
                    ins.then_inc(y_lo.sem, 1)

            def add_rows(bias):
                own.link(TT(x[:], x[:], rows4(R(bias)), ALU.add))

            def windowed(b):
                dve.wait_ge(x_in.sem, x_in.at(b, 16))
                norm(b, 0, x, y).then_inc(y_ready.sem, 1)
                split_lo(b, 0, yT)
                dve.wait_ge(ctx_in_s.sem, ctx_in_s.at(b, 16))
                moments(b, 1, ctx_tok[:, 0:NT, :])
                for j in range(2):
                    dve.wait_ge(a_proj.sem, a_proj.at(b, j + 1))
                    TS_(aff[:, j, :], ps[:, 2 + j, :], C("abq", j), float(D) ** -0.5, ALU.add, ALU.mult).then_inc(a_q.sem, 1)
                normalise(b, 1, ctx_tok[:, 0:NT, :], y).then_inc(y_ready.sem, 1)
                for j in range(7):
                    dve.wait_ge(a_hi.sem, a_hi.at(b, j + 1))
                    if j < 2:
                        ins = TT(aqT[1][:, j, :], aff[:, j, :], aqT[0][:, j, :], ALU.subtract)
                    elif j < 4:
                        ins = STT(akT[1][:, j - 2, :], ps[:, 2 + j, :], C("abk", j - 2), akT[0][:, j - 2, :], ALU.add, ALU.subtract)
                    elif j < 6:
                        t0 = 2 * (j - 4)
                        ins = TT(av[1][:, t0:t0 + 2, :].rearrange("p a n -> p (a n)"), ps[:, 2 + j, :],
                                 av[0][:, t0:t0 + 2, :].rearrange("p a n -> p (a n)"), ALU.subtract)
                    else:
                        ins = TT(av[1][:, NT, :], ps[:, 0, 0:D], av[0][:, NT, :], ALU.subtract)
                    ins.then_inc(a_lo.sem, 1)
                add_rows("abv")
                dve.wait_ge(a_scores.sem, a_scores.at(b, 1))
                own.link(TT(a_s, banks(1, 2).rearrange("p (a n) -> p a n", a=4), mask[:], ALU.add))
                V.tensor_reduce(nm[:, 0:4], a_s, AX.X, ALU.max, negate=True).then_inc(a_max.sem, 1)
                affine(b, 1, 0, CTX_AT)
                moments(b, 2, ctx_tok[:, NT:2 * NT, :])
                dve.wait_ge(a_exp.sem, a_exp.at(b, 1))
                own.link(V.reciprocal(rs[:], sums[:]))
                split_lo(b, 1, CTX_DST[0], aff_k=0)
                dve.wait_ge(a_pthi.sem, a_pthi.at(b, 1))
                TT(a_pT[1].rearrange("p a n -> p (a n)"), banks(3, 2), a_pT[0].rearrange("p a n -> p (a n)"), ALU.subtract)\
                    .then_inc(a_ptlo.sem, 1)
                normalise(b, 2, ctx_tok[:, NT:2 * NT, :], y).then_inc(y_ready.sem, 1)
                dve.wait_ge(a_out.sem, a_out.at(b, 1))
                for i in range(NT):
                    own.mark(STT(x[:, i, :], ps[:, 5 + i // 2, D * (i % 2):D * (i % 2) + D], rs[:, i:i + 1], x[:, i, :],
                                 ALU.mult, ALU.add))
                own.wait()

            def unit_lo(b, h, par, k, n):
                if k == 3:
                    dve.wait_ge(u_mm.sem, u_mm.at(b, n + 1))
                    TS_(rt_x, ps[:, 7, :], C("xbq", h), XS, ALU.add, ALU.mult).then_inc(u_q.sem, 1)
                dve.wait_ge(u_hi.sem, u_hi.at(b, n + 1))
                if k < 3:
                    sl = slice(512 * k, 512 * k + 512)
                    ins = STT(kT[par][1][:, sl], ps[:, 7, :], C("xbk", h), kT[par][0][:, sl], ALU.add, ALU.subtract)
                elif k == 3:
                    ins = TT(qT[par][1], rt_x, qT[par][0], ALU.subtract)
                elif k < 7:
                    sl = slice(4 * (k - 4), 4 * (k - 4) + 4)
                    ins = TT(v[par][1][:, sl, :].rearrange("p a n -> p (a n)"), ps[:, 7, :],
                             v[par][0][:, sl, :].rearrange("p a n -> p (a n)"), ALU.subtract)
                else:
                    ins = STT(oT[1][:, bass.ds(h, 1), :].rearrange("p a n -> p (a n)"), ps[:, 7, :], C("xbv", h),
                              oT[0][:, bass.ds(h, 1), :].rearrange("p a n -> p (a n)"), ALU.add, ALU.subtract)
                ins.then_inc(u_lo.sem, 1)

            def maxes(b, n, i):
                dve.wait_ge(s_mm.sem, s_mm.at(b, n + 1))
                V.tensor_reduce(nm[:, i:i + 1], banks(0, 3), AX.X, ALU.max, negate=True).then_inc(s_max.sem, 1)

            def head(b, h, par, last_head):
                for i in range(NT):
                    n = h * NT + i
                    for g_ in range(3):
                        dve.wait_ge(pt_hi.sem, pt_hi.at(b, 3 * n + g_ + 1))
                        sl = slice(4 * g_, 4 * g_ + 4)
                        TT(xpT[1][:, sl, :].rearrange("p a n -> p (a n)"), ps[:, 3 + g_, :],
                           xpT[0][:, sl, :].rearrange("p a n -> p (a n)"), ALU.subtract).then_inc(pt_lo.sem, 1)
                    own.mark(V.reciprocal(rs[:, i:i + 1], sums[:, i:i + 1]))
                    if i < NT - 1 or not last_head:
                        maxes(b, n + 1, (i + 1) % NT)
                    if not last_head:
                        unit_lo(b, h + 1, 1 - par, 2 * i, 7 + 8 * h + 2 * i)
                    own.wait()
                    dve.wait_ge(o_mm.sem, o_mm.at(b, n + 1))
                    TS_(on[:, i, :], ps[:, 6, P * i:P * i + P], rs[:, i:i + 1], None, ALU.mult).then_inc(o_done.sem, 1)
                    if i == NT - 1:
                        unit_lo(b, h, par, 7, 7 + 8 * h + (0 if last_head else 7))
                    elif not last_head:
                        unit_lo(b, h + 1, 1 - par, 2 * i + 1, 7 + 8 * h + 2 * i + 1)

            def latent(b):
                moments(b, 3, x)
                affine(b, 2, 1, CTX_AT)
                own.link(normalise(b, 3, x, lat))
                moments(b, 4, lat)
                split_lo(b, 2, CTX_DST[1], aff_k=1)
                normalise(b, 4, lat, y).then_inc(y_ready.sem, 1)
                for n in range(2):
                    unit_lo(b, 0, 0, FIRST[n], n)
                affine(b, 3, 2)
                split_lo(b, 3, CTX_DST[2], aff_k=2)
                for n in range(2, 7):
                    unit_lo(b, 0, 0, FIRST[n], n)
                maxes(b, 0, 0)
                with dve.Fori(0, XH // 2 - 1) as hp_:
                    own.enter(hp_, 0, 2 * NT)
                    for s_ in range(2):
                        head(b, 2 * hp_ + s_, s_, False)
                    own.leave(XH // 2 - 1)
                head(b, XH - 2, 0, False)
                head(b, XH - 1, 1, True)
                add_rows("xbo")
                dve.wait_ge(xo_mm.sem, xo_mm.at(b, 1))
                TT(x[:], banks(0, 2).rearrange("p (a n) -> p a n", a=NT), x[:], ALU.add).then_inc(xo_added.sem, 1)
                dve.wait_ge(xo_added.sem, xo_added.at(b, 1))

            def scales(k, src, scale_of_w=None):
                am, ri, sc, iv = (quant[:, k, r, :src.shape[1]] for r in range(4))
                own.link(V.tensor_reduce(am, src, AX.X, ALU.max, apply_absolute_value=True))
                own.link(TS_(am, am, 1e-5, None, ALU.max))
                own.link(V.reciprocal(ri, am))
                own.mark(TS_(sc, ri, 127.0, None, ALU.mult))
                if scale_of_w is None:
                    own.mark(TS_(iv, am, 1.0 / 127.0, None, ALU.mult))
                else:
                    own.mark(TS_(iv, am, 1.0 / 127.0, scale_of_w, ALU.mult, ALU.mult))
                own.wait()
                return sc, iv

            def bitnet(b):
                own.link(norm(b, 5, x, y))
                sc, iv = scales(0, y[:])
                for i in range(NT):
                    own.mark(TS_(y[:, i, :], y[:, i, :], sc[:, i:i + 1], ROUND, ALU.mult, ALU.add))
                own.wait()
                own.link(TS_(y[:], y[:], ROUND, 127.0, ALU.subtract, ALU.min))
                for i in range(NT):
                    last = TS_(y[:, i, :], y[:, i, :], -128.0, iv[:, i:i + 1], ALU.max, ALU.mult)
                last.then_inc(y_ready.sem, 1)
                split_lo(b, 4, yT)
                for k in range(2):
                    own.mark(V.memset(hp[:, k, 0:1], 0.0))
                    own.mark(V.memset(hp[:, k, 1 + S:2 + S], 0.0))
                own.wait()
                for m in range(NM):
                    dve.wait_ge(h_pad.sem, h_pad.at(b, m + 1))
                    if m >= 2:
                        dve.wait_ge(h_silu.sem, h_silu.at(b, m - 1))
                    q = m % 2
                    own.link(TS_(conv[:, q, 0, :], hp[:, q, 0:S], C("cw", 3 * m), C("cb", m), ALU.mult, ALU.add))
                    own.link(STT(conv[:, q, 1, :], hp[:, q, 1:1 + S], C("cw", 3 * m + 1), conv[:, q, 0, :], ALU.mult, ALU.add))
                    STT(conv[:, q, 2, :], hp[:, q, 2:2 + S], C("cw", 3 * m + 2), conv[:, q, 1, :], ALU.mult, ALU.add)\
                        .then_inc(h_conv.sem, 1)
                ivs = {}
                for i in range(NT + 1):
                    if i < NT:
                        q = i % 2
                        dve.wait_ge(g_t.sem, g_t.at(b, i + 1))
                        src = banks(4 + 2 * q, 2)
                        sc, iv = scales(q, src.unsqueeze(1), mw[:, 1:2])
                        own.link(TS_(gt[:, q, :], src, sc, ROUND, ALU.mult, ALU.add))
                        if i >= 2:
                            dve.wait_ge(gq_t.sem, gq_t.at(b, i - 1))
                        own.link(TS_(gt[:, q, :], gt[:, q, :], ROUND, -128.0, ALU.subtract, ALU.max))
                        TS_(gi[:, q, :], gt[:, q, :], 127.0, None, ALU.min).then_inc(g_quant.sem, 1)
                        ivs[i] = iv
                    if i >= 1:
                        j = i - 1
                        dve.wait_ge(f_mm.sem, f_mm.at(b, j + 1))
                        STT(x[:, j, :], ps[:, 2 + j % 2, 0:D], ivs[j], x[:, j, :], ALU.mult, ALU.add).then_inc(f_added.sem, 1)
                dve.wait_ge(f_added.sem, f_added.at(b, NT))

            def values_lo(b, n, t, bank=6):
                dve.wait_ge(lv_hi.sem, lv_hi.at(b, n + 1))
                TT(v16[:, 2 * t:2 * t + 2, :, 1 + LD:1 + 2 * LD], ps[:, bank + t % 2, :].rearrange("p (t h d) -> p t h d", t=2, d=LD),
                   v16[:, 2 * t:2 * t + 2, :, 1:1 + LD], ALU.subtract).then_inc(lv_lo.sem, 1)

            def unit_max(b, mode, it, k, ahead=0):
                kk = k + ahead
                it, kk = it + kk // 4, kk % 4
                u = mode["first"] + it * 4 + kk
                dve.wait_ge(ls_mm.sem, ls_mm.at(b, u + 1))
                src = banks(2 * (kk % 2), 2)
                if mode["heads"] == 2:
                    src = src.rearrange("p (t n) -> p t n", t=2)
                V.tensor_reduce(nm[:, 2 * kk:2 * kk + mode["heads"]], src, AX.X, ALU.max, negate=True).then_inc(ls_max.sem, 1)

            def unit_lo_l(b, mode, it, k, more):
                u = mode["first"] + it * 4 + k
                if more:
                    unit_max(b, mode, it, k, 2)
                for g_ in range(2):
                    dve.wait_ge(lt_hi.sem, lt_hi.at(b, 2 * u + g_ + 1))
                    sl = slice(4 * g_, 4 * g_ + 4)
                    TT(lpT[k % 2][1][:, sl, :].rearrange("p a n -> p (a n)"), ps[:, 4 + g_, :],
                       lpT[k % 2][0][:, sl, :].rearrange("p a n -> p (a n)"), ALU.subtract).then_inc(lt_lo.sem, 1)

            def attend(b, m_):
                mode = MODES[m_]
                nb = mode["bodies"]
                for u in range(2):
                    unit_max(b, mode, 0, u)
                with dve.Fori(0, nb - 1) as it:
                    for k in range(4):
                        unit_lo_l(b, mode, it, k, True)
                for k in range(4):
                    unit_lo_l(b, mode, nb - 1, k, k < 2)
                dve.wait_ge(lo_done.sem, lo_done.at(b, mode["body0"] + nb))
                own.mark(V.reciprocal(rl[:].rearrange("p (t h) -> p t h", t=NT), os_[:, :, :, 0]))
                yv = y[:].rearrange("p t (h d) -> p t h d", d=LD)
                own.link(TT(yv, os_[:, :, :, 1:1 + LD], os_[:, :, :, 1 + LD:1 + 2 * LD], ALU.add))
                yh = y[:].rearrange("p t (h d) -> p (t h) d", d=LD)
                TT(yh, yh, rl[:].unsqueeze(2).to_broadcast([P, NT * LH, LD]), ALU.mult).then_inc(y_ready.sem, 1)
                split_lo(b, 6 + 2 * m_, yT, bias=("sbv", "cbv")[m_])
                add_rows(("sbo", "cbo")[m_])
                dve.wait_ge(lx_mm.sem, lx_mm.at(b, m_ + 1))
                TT(x[:], banks(2, 2).rearrange("p (a n) -> p a n", a=NT), x[:], ALU.add).then_inc(lx_added.sem, 1)
                dve.wait_ge(lx_added.sem, lx_added.at(b, m_ + 1))

            def self_attention(b):
                norm(b, 6, x, y).then_inc(y_ready.sem, 1)
                split_lo(b, 5, yT)
                V.memset(v16[:, :, :, 0:1], 1.0).then_inc(ones_set.sem, 1)
                for j in range(2):
                    dve.wait_ge(lq_hi.sem, lq_hi.at(b, j + 1))
                    STT(dk[1][:, j, 0:S], ps[:, 2 + j, :], C("sbk", j), dk[0][:, j, 0:S], ALU.add, ALU.subtract).then_inc(lq_lo.sem, 1)
                for j in range(2):
                    dve.wait_ge(lq_mm.sem, lq_mm.at(b, j + 3))
                    TS_(rt[:, 0, j, :], ps[:, 4 + j, :], C("sbq", j), LD ** -0.5, ALU.add, ALU.mult).then_inc(lq_q.sem, 1)
                for j in range(2):
                    dve.wait_ge(lq_hi.sem, lq_hi.at(b, j + 3))
                    TT(dq[1][:, j, :], rt[:, 0, j, :], dq[0][:, j, :], ALU.subtract).then_inc(lq_lo.sem, 1)
                for t in range(2):
                    values_lo(b, t, t)
                for c in range(DC):
                    dve.wait_ge(cr_hi.sem, cr_hi.at(b, c + 1))
                    TT(crT[1][:, c, :], craw[:, c, :], crT[0][:, c, :], ALU.subtract).then_inc(cr_lo.sem, 1)
                attend(b, 0)

            def cross_attention(b):
                def rotate(j):
                    dve.wait_ge(rp_mm.sem, rp_mm.at(b, j + 1))
                    if j >= 2:
                        dve.wait_ge(rp_lo.sem, rp_lo.at(b, j - 1))
                    m = j - 4 if j >= 4 else j // 2
                    t0 = 512 * (j % 2)
                    tab = rope_q if j >= 4 else rope_k[:, :, t0:t0 + 512]
                    names = ("cbq", "cbqs") if j >= 4 else ("cbk", "cbks")
                    r_ = rt[:, j % 2]
                    for s_ in range(2):
                        own.mark(STT(r_[:, s_, :], ps[:, 4 + 2 * (j % 2) + s_, :], C(names[s_], m), tab[:, s_, :], ALU.add, ALU.mult))
                    own.wait()
                    TT(r_[:, 0, :], r_[:, 0, :], r_[:, 1, :], ALU.add).then_inc(rp_sum.sem, 1)

                def rotated_lo(j):
                    dve.wait_ge(rp_hi.sem, rp_hi.at(b, j + 1))
                    t0 = 512 * (j % 2)
                    hi, lo = (t[:, j - 4, :] if j >= 4 else t[:, j // 2, t0:t0 + 512] for t in (dq if j >= 4 else dk))
                    TT(lo, rt[:, j % 2, 0, :], hi, ALU.subtract).then_inc(rp_lo.sem, 1)

                moments(b, 7, x)
                rotate(0)
                normalise(b, 7, x, y).then_inc(y_ready.sem, 1)
                rotate(1)
                rotated_lo(0)
                split_lo(b, 7, yT)
                for j in range(2, 6):
                    rotate(j)
                    rotated_lo(j - 1)
                rotated_lo(5)
                for t in range(4):
                    values_lo(b, 2 + t, t, 2)
                attend(b, 1)

            def split_hidden(b, e, par):
                dve.wait_ge(e_gelu.sem, e_gelu.at(b, 2 * e + 2))
                own.link(V.tensor_copy(hgT[par][0], hg[:, par, :, :]))
                TT(hgT[par][1], hg[:, par, :, :], hgT[par][0], ALU.subtract).then_inc(e_split.sem, 1)

            def add_expert(b, e, par):
                dve.wait_ge(e_y.sem, e_y.at(b, e + 1))
                for i in range(NT):
                    last = STT(x[:, i, :], ps[:, 4 + 2 * par + i // 2, D * (i % 2):D * (i % 2) + D],
                               lg[:, 4, i, bass.ds(e, 1)], x[:, i, :], ALU.mult, ALU.add)
                last.then_inc(e_added.sem, 1)
                dve.wait_ge(e_added.sem, e_added.at(b, e + 1))

            def routed(b):
                norm(b, 8, x, y).then_inc(y_ready.sem, 1)
                split_lo(b, 9, yT)
                dve.wait_ge(r_logits.sem, r_logits.at(b, 1))
                own.link(TT(lg[:, 0], ps[:, 2, 0:NT * NE].rearrange("p (t e) -> p t e", t=NT), rows4(R("bg", NE)), ALU.add))
                own.link(V.tensor_reduce(lg[:, 1, :, 0], lg[:, 0], AX.X, ALU.max))
                own.link(TT(lg[:, 2], lg[:, 0], lg[:, 1, :, 0:1].to_broadcast([P, NT, NE]), ALU.is_ge))
                own.link(TT(lg[:, 3], lg[:, 2], rows4(R("order", NE)), ALU.mult))
                own.link(V.tensor_reduce(lg[:, 1, :, 1], lg[:, 3], AX.X, ALU.max))
                own.link(TT(lg[:, 4], lg[:, 3], lg[:, 1, :, 1:2].to_broadcast([P, NT, NE]), ALU.is_equal))
                V.tensor_copy(lg[:, 5, :, :].bitcast(F16)[:, :, 0:NE], lg[:, 4]).then_inc(r_onehot.sem, 1)
                dve.wait_ge(r_b2.sem, r_b2.at(b, 1))
                own.link(TT(x[:], banks(4, 2).rearrange("p (a n) -> p a n", a=NT), x[:], ALU.add))
                split_hidden(b, 0, 0)
                with dve.Fori(0, NE // 2 - 1) as it:
                    own.enter(it, 0, 2)
                    for s_ in range(2):
                        split_hidden(b, 2 * it + s_ + 1, 1 - s_)
                        add_expert(b, 2 * it + s_, s_)
                    own.leave(NE // 2 - 1)
                split_hidden(b, NE - 1, 1)
                add_expert(b, NE - 2, 0)
                add_expert(b, NE - 1, 1)

            with dve.Fori(0, B) as b:
                own.enter(b, 0, OWN_PER_BATCH)
                windowed(b)
                latent(b)
                bitnet(b)
                self_attention(b)
                cross_attention(b)
                routed(b)
                own.leave(B)


def chunks(w):
    k, n = w.shape
    return w.reshape(k // P, P, n).transpose(1, 0, 2).reshape(P, -1)


def columns(v_):
    return v_.reshape(-1, P).T


def swap_halves(w):
    s = w.shape
    return w.reshape(s[:-1] + (LH, 2, LD // 2))[..., ::-1, :].reshape(s)


def window_mask():
    q, c = np.arange(P)[:, None], np.arange(2 * P)[None, :]
    near = (c // BL >= q // BL) & (c // BL <= q // BL + 2)
    m = np.zeros((P, 4, 2 * P), np.float32)
    for p_ in range(4):
        token = P * p_ - BL + c
        m[:, p_, :] = np.where(near & (token >= 0) & (token < S), 0.0, -1e30)
    return m


def rope_table(n, scale):
    inv = np.float32(1.0) / np.float32(10000.0) ** (np.arange(0, LD, 2, dtype=np.float32) / np.float32(LD))
    t = np.arange(n, dtype=np.float32)
    f = np.outer(np.float32(10.0) * (t / np.float32(n)), inv).astype(np.float32)
    cos, sin = np.cos(f).T, np.sin(f).T
    c = np.tile(np.concatenate([cos, cos]), (P // LD, 1))
    s = np.tile(np.concatenate([-sin, sin]), (P // LD, 1))
    return (np.stack([c, s], 1) * scale).astype(np.float32)


def kernel(**inputs):
    import concourse.bacc as bacc
    from concourse.bass_utils import run_bass_kernel_spmd

    i = {k: np.asarray(v_) for k, v_ in inputs.items()}
    names = dict(aq="L0_attn_Wq", ak="L0_attn_Wk", av="L0_attn_Wv", xq="L0_xattn_Wq", xkv="L0_xattn_Wkv",
                 xo="L0_xattn_Wo", g="L1_ffn_Wg")
    names_t = dict(sq="L1_attn_Wq", sk="L1_attn_Wk", sv="L1_attn_Wv", so="L1_attn_Wo", cq="L1_xattn_Wq",
                   ck="L1_xattn_Wk", cv="L1_xattn_Wv", co="L1_xattn_Wo")
    w = {k: i[n] for k, n in names.items()}
    w |= {k: i[n].T for k, n in names_t.items()}
    w["cqs"], w["cks"] = swap_halves(w["cq"]), swap_halves(w["ck"])
    weights = np.concatenate([chunks(w[k]) for k, _, _ in RESIDENT], 1)
    experts = np.concatenate([chunks(i[n][e]) for e in range(NE) for n in ("L1_ffn_W1", "L1_ffn_W2")], 1)
    ternary = np.stack([chunks(i["L0_ffn_w1"].T), chunks(i["L0_ffn_w2"].T)])
    bkv = i["L0_xattn_bkv"]
    cbq, cbk = i["L1_xattn_bq"], i["L1_xattn_bk"]
    cw = i["L0_ffn_conv_w"][:, 0, :].reshape(NM, P, 3).transpose(1, 0, 2).reshape(P, -1)
    cols = [columns(i["L0_attn_bq"]), columns(i["L0_attn_bk"]), columns(i["L0_xattn_bq"]), columns(bkv[:XIN]),
            columns(bkv[XIN:]), columns(i["L0_xattn_gamma_media"]), columns(i["L0_xattn_beta_media"]),
            columns(i["L0_xattn_gamma_lat"]), columns(i["L0_xattn_beta_lat"]), cw, columns(i["L0_ffn_conv_b"]),
            columns(i["L1_attn_bq"]), columns(i["L1_attn_bk"]), columns(i["L1_attn_bv"]), columns(cbq),
            columns(swap_halves(cbq)), columns(cbk), columns(swap_halves(cbk)), columns(i["L1_xattn_bv"]),
            columns(i["L1_ffn_b1"].reshape(-1)), np.full((P, 4), -0.5, np.float32)]
    rows = np.concatenate([i["L0_attn_bv"], i["L0_xattn_bo"], i["L1_attn_bo"], i["L1_xattn_bo"], i["L1_ffn_bg"],
                           np.arange(NE, 0, -1, dtype=np.float32)])
    arrays = {
        "x": i["x"], "ctx": i["ctx_1024"], "ctx_t": i["ctx_1024"].transpose(0, 2, 1), "weights": weights,
        "experts": experts, "ternary": ternary, "cols": np.concatenate(cols, 1),
        "rows": np.broadcast_to(rows, (P, NROW)), "b2": i["L1_ffn_b2"], "window": window_mask(),
        "rope_q": rope_table(S, LD ** -0.5), "rope_k": rope_table(NCTX, 1.0),
        "eye": np.eye(P, dtype=np.float32), "eye16": np.eye(P, dtype=np.float16),
    }
    arrays = {f"in_{k}": np.ascontiguousarray(v_) for k, v_ in arrays.items()}
    nc = bacc.Bacc("TRN2", target_bir_lowering=False, num_devices=1)
    aps = [nc.dram_tensor(k, v_.shape, mybir.dt.from_np(v_.dtype), kind="ExternalInput").ap() for k, v_ in arrays.items()]
    out = nc.dram_tensor("out", (B, S, D), F32, kind="ExternalOutput").ap()
    decoder(nc, *aps, out)
    r = run_bass_kernel_spmd(nc, [arrays], core_ids=[0])
    return r.results[0]["out"]
```

```python
import concourse.bass as bass
import numpy as np
from concourse import mybir
from contextlib import ExitStack

F32 = mybir.dt.float32
F16 = mybir.dt.float16
ALU = mybir.AluOpType
ACT = mybir.ActivationFunctionType
AX = mybir.AxisListType

B, S, D = 4, 512, 256
NCTX = 1024
P = 128
NT = S // P
DC = D // P
HID = 1024
NM = HID // P
XH, XD = 8, 128
XIN = XH * XD
NKV = NCTX + S
KT_TILES = NKV // P
LH, LD = 16, 16
KR = 96
NE = 8
OWN_PER_BATCH = 189
BL = 64
ROUND = 1.5 * 2.0 ** 23

RESIDENT = [("aq", DC, D), ("ak", DC, D), ("av", DC, D), ("xq", DC, XIN), ("xkv", DC, 2 * XIN),
            ("xo", XH, D), ("sq", DC, D), ("sk", DC, D), ("sv", DC, D), ("so", DC, D),
            ("cq", DC, D), ("cqs", DC, D), ("ck", DC, D), ("cks", DC, D), ("cv", DC, D),
            ("co", DC, D), ("g", DC, NE)]
OFF, _n = {}, 0
for _name, _c, _w in RESIDENT:
    OFF[_name] = _n
    _n += _c * _w
NW = _n
WCH = 8
assert NW % WCH == 0
WC = NW // WCH
EW = 2 * DC * D

COL, _n = {}, 0
for _name, _w in [("abq", DC), ("abk", DC), ("xbq", XH), ("xbk", XH), ("xbv", XH), ("gm", DC),
                  ("bm", DC), ("gl", DC), ("bl", DC), ("cw", 3 * NM), ("cb", NM), ("sbq", DC),
                  ("sbk", DC), ("sbv", DC), ("cbq", DC), ("cbqs", DC), ("cbk", DC),
                  ("cbks", DC), ("cbv", DC), ("b1", NE * DC), ("half", 4), ("round", 1)]:
    COL[_name] = _n
    _n += _w
NCOL = _n
ROW, _n = {}, 0
for _name, _w in [("abv", D), ("xbo", D), ("sbo", D), ("cbo", D), ("bg", NE), ("order", NE)]:
    ROW[_name] = _n
    _n += _w
NROW = _n


class Signal:

    def __init__(self, nc, ctx, name, per_batch=0, credit=0):
        self.sem = ctx.enter_context(nc.semaphore(name))
        self.per_batch, self.credit = per_batch, credit

    def at(self, b, n):
        return b * self.per_batch + n + self.credit


class Order:

    def __init__(self, eng, sem):
        self.eng, self.sem, self.n, self.base, self.open = eng, sem, 0, 0, []

    def mark(self, ins):
        self.n += 1
        ins.then_inc(self.sem, 1)

    def wait(self, lag=0):
        self.eng.wait_ge(self.sem, self.base + self.n - lag)

    def link(self, ins):
        self.mark(ins)
        self.wait()

    def enter(self, i, first, per_turn):
        self.open.append((self.n, self.base, per_turn))
        self.base = self.base + (i - first) * per_turn

    def leave(self, turns):
        n, base, per_turn = self.open.pop()
        assert self.n - n == per_turn, (self.n - n, per_turn)
        self.n, self.base = n + per_turn * turns, base


def decoder(nc, x_dram, ctx_dram, ctxT_dram, w_dram, moe_in, tern_in, col_in, row_in, b2_in, mask_in,
            rope_q_in, rope_k_in, ident_in, ident16_in, out):
    c_ = ExitStack()
    with c_:
        def sb(name, shape, dt=F32):
            return c_.enter_context(nc.sbuf_tensor(name, shape, dt))

        def sig(name, per_batch=0, credit=0):
            return Signal(nc, c_, name, per_batch, credit)

        wh, wl = sb("wh", [P, NW], F16), sb("wl", [P, NW], F16)
        tern = sb("tern", [P, 2, DC * HID], F16)
        x = sb("x", [P, NT, D])
        y = sb("y", [P, NT, D])
        y_pad = (sb("yT_hi", [P, DC, S + 2 * BL], F16), sb("yT_lo", [P, DC, S + 2 * BL], F16))
        yT = tuple(t[:, :, BL:BL + S] for t in y_pad)
        akT_pad = (sb("akT_hi", [P, DC, S + 2 * BL], F16), sb("akT_lo", [P, DC, S + 2 * BL], F16))
        col = sb("col", [P, NCOL])
        row = sb("row", [P, NROW])
        b2 = sb("b2", [NE, D])
        b2h, b2l = sb("b2h", [NE, D], F16), sb("b2l", [NE, D], F16)
        mask = sb("mask", [P, 4, 2 * P])
        rope_q = sb("rope_q", [P, 2, S])
        rope_k = sb("rope_k", [P, 2, NCTX])
        ident = sb("ident", [P, P])
        ident16 = sb("ident16", [P, P], F16)
        ones = sb("ones", [P, P])
        st = sb("st", [P, NT, 6])
        mv = sb("mv", [P, NT, 2])
        ve = sb("ve", [P, NT])
        rstd = sb("rstd", [P, NT])
        quant = sb("quant", [P, 2, 4, NT])
        wsum = sb("wsum", [P, 2])
        mw = sb("mw", [P, 2])
        msc = sb("msc", [P, 2])
        nm = sb("nm", [P, 8])
        sums = sb("sums", [P, 4])
        rs = sb("rs", [P, 4])
        rl = sb("rl", [P, NT * LH])
        warm = sb("warm", [P, 4])

        ARENA = 97 * 1024
        arena = sb("arena", [P, ARENA // 4])

        class Layout:
            def __init__(self, at=0):
                self.at = at

            def take(self, shape, dt=F32):
                n = int(np.prod(shape)) * (4 if dt == F32 else 2)
                assert n % 4 == 0 and self.at + n <= ARENA, (self.at, n)
                v = arena[:, self.at // 4:(self.at + n) // 4]
                self.at += n
                if dt != F32:
                    v = v.bitcast(dt)
                names = "abcd"[:len(shape)]
                if len(shape) > 1:
                    v = v.rearrange("p (" + " ".join(names) + ") -> p " + " ".join(names),
                                    **{k: s for k, s in zip(names, shape)})
                return v

            def pair(self, shape):
                return self.take(shape, F16), self.take(shape, F16)

        lay = Layout()
        stage = lay.take([2, EW * 2])
        est = [lay.pair([2 * EW]) for _ in range(2)]
        tstage = [lay.take([DC * HID]) for _ in range(2)]
        lay = Layout()
        ctx_tok = lay.take([NCTX // P, D])
        cT = lay.pair([DC, NKV])
        heads_at = lay.at
        av = lay.pair([NT + 1, D])
        lay = Layout(heads_at + 4 * NKV)
        aff = lay.take([2, S])
        aqT = lay.pair([DC, S])
        akT = tuple(t[:, :, BL:BL + S] for t in akT_pad)
        a_s = lay.take([4, 2 * P])
        a_p = lay.take([4, 2 * P])
        lat = lay.take([NT, D])
        a_pT = lay.pair([8, P])
        assert lay.at <= heads_at + 40 * 1024
        lay = Layout(heads_at)
        kT = [lay.pair([NKV]) for _ in range(2)]
        qT = [lay.pair([S]) for _ in range(2)]
        v = [lay.pair([KT_TILES, P]) for _ in range(2)]
        xp = lay.take([NKV])
        xpT = lay.pair([KT_TILES, P])
        rt_x = lay.take([S])
        on = lay.take([NT, P])
        oT = lay.pair([XH, S])
        lay = Layout()
        hp = lay.take([3, S + 2])
        conv = lay.take([2, 3, S])
        g = lay.take([NM, S])
        gt = lay.take([2, HID])
        gi = lay.take([2, HID], F16)
        gq = lay.take([NM, S], F16)
        lay = Layout()
        qs = lay.take([LH, S], F16)
        ks = lay.take([LH, NCTX], F16)
        VW = 2 * LD + 2
        v16 = lay.take([NCTX // P, LH, VW], F16)
        os_at = lay.at
        os_ = lay.take([NT, LH, VW])
        lp = lay.take([2, 1024])
        lpT = [lay.pair([8, P]) for _ in range(2)]
        crT = lay.pair([DC, NCTX])
        craw = lay.take([DC, NCTX])
        lay = Layout(os_at)
        dq = lay.pair([DC, S])
        dk = lay.pair([DC, NCTX])
        rt = lay.take([2, 2, S])
        assert lay.at <= os_at + 4 * (NT * LH * VW + 2048) + 4096
        lay = Layout()
        ew = lay.take([2, NE * EW], F16)
        hg = lay.take([2, DC, S])
        hgT = [lay.pair([DC, S]) for _ in range(2)]
        lg = lay.take([6, NT, NE])
        mT = lay.take([S], F16)

        ps = c_.enter_context(nc.psum_tensor("ps", [P, 8, 512], F32))

        def banks(k, n):
            return ps[:, k:k + n, :].rearrange("p k n -> p (k n)")

        ew_d = nc.dram_tensor("ew_d", (2, P, NE * EW), F16, kind="Internal").ap()
        qd = nc.dram_tensor("qd", (2, D, S), F16, kind="Internal").ap()
        kd = nc.dram_tensor("kd", (2, D, NCTX), F16, kind="Internal").ap()

        const_in, pads_set = sig("const_in"), sig("pads_set")
        w_in = [sig(f"w_in{i}") for i in range(2)]
        w_hi, w_lo = sig("w_hi"), sig("w_lo", 0, 1)
        ew_out = [sig(f"ew_out{i}", 0, 1) for i in range(2)]
        t_in, t_sum, t_all, t_done = sig("t_in"), sig("t_sum"), sig("t_all"), sig("t_done")
        y_in = sig("y_in", 16)
        x_in, ctx_in_s, craw_in, ew_in = (sig("x_in", 16), sig("ctx_in", 16), sig("craw_in", 16),
                                          sig("ew_in", 32))
        x_out = sig("x_out", 16, 1)
        k_out, q_out = sig("k_out", 8 * 16), sig("q_out", 8 * 16)
        qk_in = [sig(f"qk_in{c}", 12 * 16) for c in range(DC)]
        var_ready, rstd_ready = sig("var_ready", 9), sig("rstd_ready", 9)
        y_ready, y_t, y_hi, y_lo = sig("y_ready", 10), sig("y_t", 20, 1), sig("y_hi", 20), sig("y_lo", 20)
        aff_done, y_half = sig("aff_done", 6), sig("y_half", 2)
        a_proj, a_q, a_hi, a_lo = sig("a_proj", 7), sig("a_q", 2), sig("a_hi", 7), sig("a_lo", 7)
        a_scores, a_max, a_exp = sig("a_scores", 1), sig("a_max", 1), sig("a_exp", 1)
        a_pt, a_pthi, a_ptlo, a_out = sig("a_pt", 1), sig("a_pthi", 1), sig("a_ptlo", 1), sig("a_out", 1)
        NU = 8 * XH
        NTI = NT * XH
        u_mm, u_hi, u_lo, u_q = sig("u_mm", NU), sig("u_hi", NU), sig("u_lo", NU, 1), sig("u_q", XH)
        s_mm, s_max, s_exp = sig("s_mm", NTI), sig("s_max", NTI), sig("s_exp", NTI)
        pt_mm, pt_hi, pt_lo = sig("pt_mm", 3 * NTI), sig("pt_hi", 3 * NTI), sig("pt_lo", 3 * NTI)
        o_mm, o_done = sig("o_mm", NTI), sig("o_done", NTI, 1)
        xo_mm, xo_added = sig("xo_mm", 1), sig("xo_added", 1)
        h_mm, h_pad, h_conv, h_silu = sig("h_mm", NM), sig("h_pad", NM), sig("h_conv", NM), sig("h_silu", NM)
        g_scale, g_scaled = sig("g_scale", NT), sig("g_scaled", NT)
        g_t, g_quant, gq_t, gq_done = sig("g_t", NT), sig("g_quant", NT), sig("gq_t", NT), sig("gq_done", NT)
        f_mm, f_added = sig("f_mm", NT), sig("f_added", NT)
        lq_mm, lq_q, lq_hi, lq_lo = sig("lq_mm", 4), sig("lq_q", 2), sig("lq_hi", 4), sig("lq_lo", 4)
        rows_zero = sig("rows_zero", 2)
        cr_hi, cr_lo = sig("cr_hi", DC), sig("cr_lo", DC)
        rp_mm, rp_mul, rp_sum, rp_hi, rp_lo = sig("rp_mm", 6), sig("rp_mul", 6), sig("rp_sum", 6), sig("rp_hi", 6), sig("rp_lo", 6, 1)
        lv_mm, lv_hi, lv_lo = sig("lv_mm", 6), sig("lv_hi", 6), sig("lv_lo", 6)
        ones_set = sig("ones_set", 1)
        UD, UE = 32, 64
        UN = UD + UE
        ls_mm, ls_max, ls_exp = sig("ls_mm", UN), sig("ls_max", UN), sig("ls_exp", UN)
        lt_mm, lt_hi, lt_lo = sig("lt_mm", 2 * UN), sig("lt_hi", 2 * UN), sig("lt_lo", 2 * UN)
        lo_mm, lo_done = sig("lo_mm", UN), sig("lo_done", UN // 4, 1)
        lx_mm, lx_added = sig("lx_mm", 2 * NT), sig("lx_added", 2 * NT)
        r_logits, r_onehot, r_oT, r_mT, r_b2 = (sig("r_logits", 1), sig("r_onehot", 1), sig("r_oT", 1),
                                               sig("r_mT", 1), sig("r_b2", 1))
        e_h, e_gelu, e_split, e_y, e_added = (sig("e_h", 2 * NE), sig("e_gelu", 2 * NE),
                                              sig("e_split", NE, 1), sig("e_y", NE), sig("e_added", NE, 1))
        dve_own = sig("dve_own")
        passed = sig("passed")

        def W(name, c, n0, n):
            width = next(w_ for k_, _, w_ in RESIDENT if k_ == name)
            at = OFF[name] + c * width + n0
            return wh[:, bass.ds(at, n)], wl[:, bass.ds(at, n)]

        def C(name, i=0):
            return col[:, bass.ds(COL[name] + i, 1)]

        def R(name, n=D):
            return row[:, ROW[name]:ROW[name] + n]

        def both(pair, *at):
            return tuple(t[at] for t in pair)

        def rows4(v_, n=NT):
            return v_.unsqueeze(1).to_broadcast([P, n, v_.shape[-1]])

        def alone(eng):
            eng.sem_inc(passed.sem, 1)

        CTX_AT = (7, 0)
        FIRST = (0, 1, 4, 5, 2, 3, 6)
        CTX_DST = [both(cT, slice(None), slice(None), slice(512 * k, 512 * k + 512)) for k in range(3)]
        FIRST_BANK = (6, 5, 4, 3, 7, 2, 6)
        TILE_BANK = (2, 3, 0, 1)
        XS = float(np.float32(XD ** -0.5))
        MODES = [dict(nk=S, heads=2, bodies=8, first=0, body0=0), dict(nk=NCTX, heads=1, bodies=16, first=UD, body0=8)]

        block = c_.enter_context(nc.Block())

        @block.sync
        def _(sp):
            for signal in (x_out, *ew_out):
                sp.sem_inc(signal.sem, 1)
            consts = [(col, col_in), (row, row_in), (b2, b2_in), (mask, mask_in), (rope_q, rope_q_in),
                      (rope_k, rope_k_in), (ident, ident_in), (ident16, ident16_in)]
            for dst, src in consts:
                sp.dma_start(dst[:], src).then_inc(const_in.sem, 16)
            for k in range(2):
                sp.dma_start(tstage[k], tern_in[k]).then_inc(t_in.sem, 16)
            with sp.Fori(0, WCH // 2) as it:
                for s_ in range(2):
                    sp.wait_ge(w_lo.sem, w_lo.at(0, 2 * it))
                    alone(sp)
                    sp.dma_start(stage[:, s_, 0:WC], w_dram[:, bass.ds((2 * it + s_) * WC, WC)]).then_inc(w_in[s_].sem, 16)
            with sp.Fori(0, 2) as it:
                for s_ in range(2):
                    sp.wait_ge(w_lo.sem, w_lo.at(0, WCH + 2 * it))
                    alone(sp)
                    sp.dma_start(stage[:, s_, :], moe_in[:, bass.ds(it * 4 * EW + s_ * 2 * EW, 2 * EW)])\
                      .then_inc(w_in[s_].sem, 16)
                for s_ in range(2):
                    sp.wait_ge(w_lo.sem, w_lo.at(0, WCH + 2 * it + s_ + 1))
                    alone(sp)
                    for part in range(2):
                        sp.dma_start(ew_d[part, :, bass.ds(it * 4 * EW + s_ * 2 * EW, 2 * EW)],
                                     est[s_][part]).then_inc(ew_out[s_].sem, 16)
            sp.wait_ge(w_lo.sem, w_lo.at(0, WCH + 4))
            for s_ in range(2):
                sp.wait_ge(ew_out[s_].sem, ew_out[s_].at(0, 64))
            sp.wait_ge(t_done.sem, 2)
            with sp.Fori(0, B) as b:
                sp.wait_ge(x_out.sem, x_out.at(b, 0))
                alone(sp)
                sp.dma_start(x[:], x_dram[bass.ds(b, 1)].rearrange("b (i p) d -> p (b i) d", p=P)).then_inc(x_in.sem, 16)
                sp.wait_ge(e_added.sem, e_added.at(b, 0))
                alone(sp)
                sp.dma_start(ctx_tok, ctx_dram[bass.ds(b, 1)].rearrange("b (i p) d -> p (b i) d", p=P)).then_inc(ctx_in_s.sem, 16)
                sp.wait_ge(xo_added.sem, xo_added.at(b, 1))
                alone(sp)
                sp.dma_start(craw, ctxT_dram[bass.ds(b, 1)].rearrange("b (c p) t -> p (b c) t", p=P)).then_inc(craw_in.sem, 16)
                def send(split, d_, src, n, c, done):
                    sp.wait_ge(split[0].sem, split[0].at(b, split[1]))
                    alone(sp)
                    for part in range(2):
                        sp.dma_start(d_[part, P * c:P * c + P, 0:n], src[part][:, c, 0:n]).then_inc(done.sem, 16)

                def stack(sent, count, d_, heads, n, c):
                    sp.wait_ge(sent.sem, sent.at(b, 16 * count))
                    alone(sp)
                    sp.wait_ge(rows_zero.sem, rows_zero.at(b, 2))
                    alone(sp)
                    for r_, part in enumerate((0, 1, 0) if d_ is qd else (0, 0, 1)):
                        sp.dma_start(heads[16 * r_:16 * r_ + 16, P // LD * c:P // LD * c + P // LD, 0:n],
                                     d_[part, P * c:P * c + P, 0:n].rearrange("(h d) t -> d h t", d=LD))\
                          .then_inc(qk_in[c].sem, 16)

                for c in range(DC):
                    send((lq_lo, 2 * c + 1), kd, dk, S, c, k_out)
                    send((lq_lo, 2 * c + 2), qd, dq, S, c, q_out)
                    stack(k_out, 2 * c + 2, kd, ks, S, c)
                    stack(q_out, 2 * c + 2, qd, qs, S, c)
                send((rp_lo, 2), kd, dk, NCTX, 0, k_out)
                sp.wait_ge(ls_mm.sem, ls_mm.at(b, UD))
                alone(sp)
                stack(k_out, 6, kd, ks, NCTX, 0)
                send((rp_lo, 4), kd, dk, NCTX, 1, k_out)
                send((rp_lo, 5), qd, dq, S, 0, q_out)
                stack(q_out, 6, qd, qs, S, 0)
                send((rp_lo, 6), qd, dq, S, 1, q_out)
                stack(k_out, 8, kd, ks, NCTX, 1)
                stack(q_out, 8, qd, qs, S, 1)
                sp.wait_ge(ls_mm.sem, ls_mm.at(b, UN))
                for part in range(2):
                    sp.dma_start(ew[:, part, :], ew_d[part]).then_inc(ew_in.sem, 16)
                sp.wait_ge(e_added.sem, e_added.at(b, NE))
                alone(sp)
                sp.dma_start(out[bass.ds(b, 1)].rearrange("b (i p) d -> p (b i) d", p=P), x[:]).then_inc(x_out.sem, 16)
            sp.wait_ge(x_out.sem, x_out.at(B, 0))

        @block.gpsimd
        def _(pool):
            def zero_rows(t):
                nc.gpsimd.memset(t[0:KR].rearrange("p h t -> p (h t)").bitcast(F32), 0.0).then_inc(rows_zero.sem, 1)

            nc.gpsimd.memset(ones[:], 1.0).then_inc(pads_set.sem, 1)
            for t in (*y_pad, *akT_pad):
                nc.gpsimd.memset(t[:, :, 0:BL], 0.0).then_inc(pads_set.sem, 1)
                nc.gpsimd.memset(t[:, :, BL + S:], 0.0).then_inc(pads_set.sem, 1)
            pool.wait_ge(const_in.sem, 16 * 8)
            def add_rotated(b, j):
                pool.wait_ge(rp_mul.sem, rp_mul.at(b, j + 1))
                nc.gpsimd.tensor_tensor(rt[:, j % 2, 0, :], rt[:, j % 2, 0, :], rt[:, j % 2, 1, :], ALU.add)\
                  .then_inc(rp_sum.sem, 1)

            with pool.Fori(0, B) as b:
                pool.wait_ge(y_t.sem, y_t.at(b, 0))
                alone(pool)
                pool.dma_start(y[:], x_dram[bass.ds(b, 1)].rearrange("b (i p) d -> p (b i) d", p=P)).then_inc(y_in.sem, 16)
                for k in range(9):
                    if k == 6:
                        pool.wait_ge(h_silu.sem, h_silu.at(b, NM))
                        alone(pool)
                        zero_rows(qs)
                    if k == 7:
                        add_rotated(b, 0)
                    pool.wait_ge(var_ready.sem, var_ready.at(b, k + 1))
                    nc.gpsimd.tensor_tensor(rstd[:], ve[:], col[:, COL["half"]:COL["half"] + NT], ALU.pow)\
                      .then_inc(rstd_ready.sem, 1)
                    if k == 6:
                        zero_rows(ks)
                    if k == 7:
                        for j in range(1, 4):
                            add_rotated(b, j)

        @block.tensor
        def _(pe):
            mm = nc.tensor.matmul
            pe.sem_inc(y_t.sem, 1)

            def product(out_, pairs):
                last, n = None, len(pairs)
                for k, ((lh, ll), (rh, rl_)) in enumerate(pairs):
                    mm(out_, lh, rh, start=(k == 0), stop=False)
                    mm(out_, lh, rl_, start=False, stop=False)
                    last = mm(out_, ll, rh, start=False, stop=(k == n - 1))
                return last

            def keep_warm(n, bank):
                for _ in range(n):
                    mm(ps[:, bank, :], ident16[:], wh[:, 0:512], start=True, stop=True)

            def transpose_y(b, k, at=(0, 1), half=None):
                if half is None:
                    pe.wait_ge(y_ready.sem, y_ready.at(b, k + 1))
                for c in range(DC):
                    if half is not None:
                        pe.wait_ge(*((y_half.sem, y_half.at(b, half + 1)) if c == 0 else (y_ready.sem, y_ready.at(b, k + 1))))
                    for i in range(NT):
                        last = nc.tensor.transpose(ps[:, at[c], P * i:P * i + P], y[:, i, P * c:P * c + P], ident[:])
                    last.then_inc(y_t.sem, 1)

            pe.wait_ge(pads_set.sem, 9)
            pe.wait_ge(t_sum.sem, 2)
            mm(ps[:, 0, 0:2], ones[:], wsum[:], start=True, stop=True).then_inc(t_all.sem, 1)
            pe.wait_ge(t_done.sem, 2)
            pe.wait_ge(w_lo.sem, w_lo.at(0, WCH + 4))
            pe.wait_ge(const_in.sem, 16 * 8)

            def windowed(b):
                pe.wait_ge(var_ready.sem, var_ready.at(b, 1))
                keep_warm(8, 3)
                transpose_y(b, 0)
                pe.wait_ge(y_lo.sem, y_lo.at(b, 2))
                for j, (name, m) in enumerate([("aq", 0), ("aq", 1), ("ak", 0), ("ak", 1)]):
                    product(ps[:, 2 + j, :], [(W(name, c, P * m, P), both(yT, slice(None), c)) for c in range(DC)])\
                        .then_inc(a_proj.sem, 1)
                for j in range(NT + 1):
                    last = product(ps[:, (6, 6, 7, 7, 0)[j], D * (j % 2):D * (j % 2) + D],
                                   [(both(y_pad, slice(None), c, slice(P * j, P * j + P)), W("av", c, 0, D))
                                    for c in range(DC)])
                    if j % 2 or j == NT:
                        last.then_inc(a_proj.sem, 1)
                pe.wait_ge(a_lo.sem, a_lo.at(b, 4))
                for p_ in range(4):
                    last = product(ps[:, 1 + p_ // 2, 256 * (p_ % 2):256 * (p_ % 2) + 256],
                                   [(both(aqT, slice(None), c, slice(P * p_, P * p_ + P)),
                                     both(akT_pad, slice(None), c, slice(P * p_, P * p_ + 2 * P))) for c in range(DC)])
                last.then_inc(a_scores.sem, 1)
                pe.wait_ge(a_lo.sem, a_lo.at(b, 7))
                transpose_y(b, 1, CTX_AT)
                keep_warm(12, 6)
                pe.wait_ge(a_exp.sem, a_exp.at(b, 1))
                for n in range(8):
                    last = nc.tensor.transpose(ps[:, 3 + n // 4, P * (n % 4):P * (n % 4) + P],
                                               a_p[:, n // 2, P * (n % 2):P * (n % 2) + P], ident[:])
                last.then_inc(a_pt.sem, 1)
                keep_warm(8, 6)
                pe.wait_ge(a_ptlo.sem, a_ptlo.at(b, 1))
                for p_ in range(4):
                    last = product(ps[:, 5 + p_ // 2, 256 * (p_ % 2):256 * (p_ % 2) + 256],
                                   [(both(a_pT, slice(None), 2 * p_ + kc), both(av, slice(None), p_ + kc))
                                    for kc in range(2)])
                last.then_inc(a_out.sem, 1)
                transpose_y(b, 2, CTX_AT)

            def unit(b, h, par, k, free, bank=7):
                if free is not None:
                    pe.wait_ge(u_lo.sem, u_lo.at(b, free))
                if k < 3:
                    last = product(ps[:, bank, :], [(W("xkv", c, h * XD, XD), both(cT, slice(None), c, slice(512 * k, 512 * k + 512)))
                                                 for c in range(DC)])
                elif k == 3:
                    last = product(ps[:, bank, :], [(W("xq", c, h * XD, XD), both(cT, slice(None), c, slice(NCTX, NKV)))
                                                 for c in range(DC)])
                else:
                    for t in range(4):
                        a0 = P * (4 * (k - 4) + t)
                        last = product(ps[:, bank, P * t:P * t + P],
                                       [(both(cT, slice(None), c, slice(a0, a0 + P)), W("xkv", c, h * XD + XIN, XD))
                                        for c in range(DC)])
                last.then_inc(u_mm.sem, 1)

            def scores(b, par, i):
                for t in range(3):
                    last = product(ps[:, t, :], [(both(qT[par], slice(None), slice(P * i, P * i + P)),
                                                  both(kT[par], slice(None), slice(512 * t, 512 * t + 512)))])
                last.then_inc(s_mm.sem, 1)

            def project(tiles, heads):
                for i in tiles:
                    for h in heads:
                        (oh, ol), (wh_, wl_) = both(oT, slice(None), h, slice(P * i, P * i + P)), W("xo", h, 0, D)
                        d_ = ps[:, i, 0:D]
                        mm(d_, oh, wh_, start=(h == 0), stop=False)
                        mm(d_, oh, wl_, start=False, stop=False)
                        last = mm(d_, ol, wh_, start=False, stop=(h == XH - 1))
                return last

            def head(b, h, par, last_head):
                for i in range(NT):
                    n = h * NT + i
                    pe.wait_ge(s_exp.sem, s_exp.at(b, n + 1))
                    for g_ in range(3):
                        for t in range(4):
                            kt = 4 * g_ + t
                            last = nc.tensor.transpose(ps[:, 3 + g_, P * t:P * t + P], xp[:, P * kt:P * kt + P], ident[:])
                        last.then_inc(pt_mm.sem, 1)
                    if i < NT - 1:
                        scores(b, par, i + 1)
                    elif not last_head:
                        pe.wait_ge(u_lo.sem, u_lo.at(b, 7 + 8 * h + 4))
                        scores(b, 1 - par, 0)
                    k = 2 * i
                    if not last_head:
                        unit(b, h + 1, 1 - par, k, 7 + 8 * h + k)
                    elif i == NT - 1:
                        pe.wait_ge(u_lo.sem, u_lo.at(b, 7 + 8 * h))
                        project(range(3), range(XH - 1))
                    pe.wait_ge(pt_lo.sem, pt_lo.at(b, 3 * (n + 1)))
                    pe.wait_ge(o_done.sem, o_done.at(b, n))
                    if i == 0:
                        pe.wait_ge(u_lo.sem, u_lo.at(b, 7 + 8 * h - 0) if not last_head else u_lo.at(b, 7 + 8 * h))
                    product(ps[:, 6, P * i:P * i + P],
                            [(both(xpT, slice(None), kt), both(v[par], slice(None), kt)) for kt in range(KT_TILES)])\
                        .then_inc(o_mm.sem, 1)
                    k = 2 * i + 1
                    if k < 7:
                        if not last_head:
                            unit(b, h + 1, 1 - par, k, 7 + 8 * h + k)
                    else:
                        if last_head:
                            project(range(3, NT), range(XH - 1))
                        before = 7 + 8 * h + (0 if last_head else 7)
                        pe.wait_ge(u_lo.sem, u_lo.at(b, before))
                        pe.wait_ge(o_done.sem, o_done.at(b, n + 1))
                        for t in range(NT):
                            last = nc.tensor.transpose(ps[:, 7, P * t:P * t + P], on[:, t, :], ident[:])
                        last.then_inc(u_mm.sem, 1)

            def latent(b):
                pe.wait_ge(var_ready.sem, var_ready.at(b, 4))
                keep_warm(16, 3)
                pe.wait_ge(y_lo.sem, y_lo.at(b, 6))
                for n in range(2):
                    unit(b, 0, 0, FIRST[n], 1 if n == 6 else None, FIRST_BANK[n])
                transpose_y(b, 3)
                for n in range(2, 7):
                    if n == 4:
                        pe.wait_ge(y_lo.sem, y_lo.at(b, 8))
                    unit(b, 0, 0, FIRST[n], 1 if n == 6 else None, FIRST_BANK[n])
                pe.wait_ge(u_lo.sem, u_lo.at(b, 6))
                scores(b, 0, 0)
                with pe.Fori(0, XH // 2 - 1) as hp_:
                    for s_ in range(2):
                        head(b, 2 * hp_ + s_, s_, False)
                head(b, XH - 2, 0, False)
                head(b, XH - 1, 1, True)
                pe.wait_ge(u_lo.sem, u_lo.at(b, NU))
                project(range(NT), (XH - 1,)).then_inc(xo_mm.sem, 1)

            def bitnet(b):
                pe.wait_ge(var_ready.sem, var_ready.at(b, 6))
                keep_warm(24, 4)
                transpose_y(b, 4)
                pe.wait_ge(y_lo.sem, y_lo.at(b, 10))

                def early_transposes(m):
                    pe.wait_ge(h_silu.sem, h_silu.at(b, m + 1))
                    for i in range(2):
                        last = nc.tensor.transpose(ps[:, 4 + 2 * i + m // 4, P * (m % 4):P * (m % 4) + P],
                                                   g[:, m, P * i:P * i + P], ident[:])
                        if m == NM - 1:
                            last.then_inc(g_t.sem, 1)

                for m in range(NM):
                    if m >= 2:
                        pe.wait_ge(h_pad.sem, h_pad.at(b, m - 1))
                    for c in range(DC):
                        for part in range(2):
                            last = mm(ps[:, 2 + m % 2, :], tern[:, 0, HID * c + P * m:HID * c + P * m + P],
                                      yT[part][:, c, :], start=(c + part == 0), stop=(c + part == 2))
                    last.then_inc(h_mm.sem, 1)
                    if m >= 3:
                        early_transposes(m - 3)
                for m in range(NM - 3, NM):
                    early_transposes(m)
                for i in range(2, NT):
                    pe.wait_ge(g_scaled.sem, g_scaled.at(b, i - 1))
                    for m in range(NM):
                        last = nc.tensor.transpose(ps[:, 4 + 2 * (i % 2) + m // 4, P * (m % 4):P * (m % 4) + P],
                                                   g[:, m, P * i:P * i + P], ident[:])
                    last.then_inc(g_t.sem, 1)
                for j in range(NT + 1):
                    if j < NT:
                        pe.wait_ge(g_quant.sem, g_quant.at(b, j + 1))
                        if j >= 2:
                            pe.wait_ge(gq_done.sem, gq_done.at(b, j - 1))
                        dst = ps[:, j % 2, :].bitcast(F16)
                        for m in range(NM):
                            last = nc.tensor.transpose(dst[:, P * m:P * m + P], gi[:, j % 2, P * m:P * m + P], ident16[:])
                        last.then_inc(gq_t.sem, 1)
                    if j >= 1:
                        i = j - 1
                        pe.wait_ge(gq_done.sem, gq_done.at(b, i + 1))
                        if i >= 2:
                            pe.wait_ge(f_added.sem, f_added.at(b, i - 1))
                        for m in range(NM):
                            last = mm(ps[:, 2 + i % 2, 0:D], gq[:, m, P * i:P * i + P], tern[:, 1, D * m:D * m + D],
                                      start=(m == 0), stop=(m == NM - 1))
                        last.then_inc(f_mm.sem, 1)

            def unit_scores(b, mode, it, k, ahead=0):
                kk = k + ahead
                it, kk = it + kk // 4, kk % 4
                u = mode["first"] + it * 4 + kk
                if not (isinstance(it, int) and it == 0 and kk < 2):
                    pe.wait_ge(ls_exp.sem, ls_exp.at(b, u - 1))
                for t in range(2):
                    if mode["heads"] == 2:
                        h, i, k0 = 2 * it + kk // 2, 2 * (kk % 2) + t, 0
                    else:
                        h, i, k0 = it, kk, 512 * t
                    last = mm(ps[:, 2 * (kk % 2) + t, :], qs[0:KR, bass.ds(h, 1), P * i:P * i + P].rearrange("p a n -> p (a n)"),
                              ks[0:KR, bass.ds(h, 1), k0:k0 + 512].rearrange("p a n -> p (a n)"), start=True, stop=True)
                last.then_inc(ls_mm.sem, 1)

            def unit_transpose(b, mode, it, k, ahead=0):
                kk = k + ahead
                it, kk = it + kk // 4, kk % 4
                u = mode["first"] + it * 4 + kk
                pe.wait_ge(ls_exp.sem, ls_exp.at(b, u + 1))
                for g_ in range(2):
                    if not (isinstance(it, int) and it + kk == 0):
                        pe.wait_ge(lt_lo.sem, lt_lo.at(b, 2 * u - 1 + g_))
                    for t in range(4):
                        n = 4 * g_ + t
                        last = nc.tensor.transpose(ps[:, 4 + g_, P * t:P * t + P], lp[:, kk % 2, P * n:P * n + P], ident[:])
                    last.then_inc(lt_mm.sem, 1)

            def unit_out(b, mode, it, k):
                u = mode["first"] + it * 4 + k
                pe.wait_ge(lt_lo.sem, lt_lo.at(b, 2 * (u + 1)))
                if k == 0:
                    pe.wait_ge(lo_done.sem, lo_done.at(b, mode["body0"] + it))
                two = mode["heads"] == 2
                nkt = mode["nk"] // P
                for t in range(2 if two else 1):
                    i = 2 * (k % 2) + t if two else k
                    h = 2 * it + k // 2 if two else it
                    o0 = (i * 2 + k // 2) * VW if two else i * VW
                    for kt in range(nkt):
                        n = t * nkt + kt
                        hi, lo = (part[:, n, :] for part in lpT[k % 2])
                        mm(ps[:, 6, o0:o0 + VW - 1], hi,
                           v16[:, kt, bass.ds(h, 1), 0:VW - 1].rearrange("p a n -> p (a n)"), start=(kt == 0), stop=False)
                        last = mm(ps[:, 6, o0:o0 + 1 + LD], lo,
                                  v16[:, kt, bass.ds(h, 1), 0:1 + LD].rearrange("p a n -> p (a n)"), start=False, stop=(kt == nkt - 1))
                last.then_inc(lo_mm.sem, 1)

            def attend(b, m_):
                mode = MODES[m_]
                pe.wait_ge(lv_lo.sem, lv_lo.at(b, (2, 6)[m_]))
                pe.wait_ge(qk_in[0].sem, qk_in[0].at(b, 96 * (m_ + 1)))
                for u in range(3):
                    unit_scores(b, mode, 0, u)
                nb = mode["bodies"]
                unit_transpose(b, mode, 0, 0)
                unit_scores(b, mode, 0, 3)
                for i0, i1 in ((0, nb // 2 - 1), (nb // 2 - 1, nb - 1)):
                    if i0:
                        pe.wait_ge(qk_in[1].sem, qk_in[1].at(b, 96 * (m_ + 1)))
                        alone(pe)
                    with pe.Fori(i0, i1) as it:
                        for k in range(4):
                            unit_transpose(b, mode, it, k, 1)
                            unit_scores(b, mode, it, k, 4)
                            unit_out(b, mode, it, k)
                for k in range(4):
                    if k < 3:
                        unit_transpose(b, mode, nb - 1, k, 1)
                    unit_out(b, mode, nb - 1, k)
                if m_ == 0:
                    pe.wait_ge(cr_lo.sem, cr_lo.at(b, DC))
                    rope_product(b, 0)
                else:
                    keep_warm(12, 0)
                transpose_y(b, 6 + 2 * m_, half=m_)
                if m_ == 0:
                    rope_product(b, 1)
                pe.wait_ge(y_lo.sem, y_lo.at(b, 2 * (7 + 2 * m_)))
                for i in range(NT):
                    product(ps[:, TILE_BANK[i], 0:D],
                            [(both(yT, slice(None), c, slice(P * i, P * i + P)), W(("so", "co")[m_], c, 0, D))
                             for c in range(DC)]).then_inc(lx_mm.sem, 1)

            def self_attention(b):
                pe.wait_ge(var_ready.sem, var_ready.at(b, 7))
                keep_warm(8, 4)
                transpose_y(b, 5)
                pe.wait_ge(y_lo.sem, y_lo.at(b, 12))
                for j, (name, m) in enumerate([("sk", 0), ("sq", 0), ("sk", 1), ("sq", 1)]):
                    product(ps[:, 2 + j, :], [(W(name, c, P * m, P), both(yT, slice(None), c)) for c in range(DC)])\
                        .then_inc(lq_mm.sem, 1)
                for i in range(NT):
                    last = product(ps[:, 6 + i // 2, D * (i % 2):D * (i % 2) + D],
                                   [(both(yT, slice(None), c, slice(P * i, P * i + P)), W("sv", c, 0, D)) for c in range(DC)])
                    if i % 2:
                        last.then_inc(lv_mm.sem, 1)
                attend(b, 0)

            def rope_product(b, j):
                if j >= 2:
                    pe.wait_ge(rp_mul.sem, rp_mul.at(b, j - 1))
                m = j - 4 if j >= 4 else j // 2
                t0 = 512 * (j % 2)
                src = [both(yT, slice(None), c) if j >= 4 else both(crT, slice(None), c, slice(t0, t0 + 512)) for c in range(DC)]
                for s_, name in enumerate((("cq", "cqs") if j >= 4 else ("ck", "cks"))):
                    last = product(ps[:, 4 + 2 * (j % 2) + s_, :], [(W(name, c, P * m, P), src[c]) for c in range(DC)])
                last.then_inc(rp_mm.sem, 1)

            def cross_attention(b):
                for j in range(2, 6):
                    if j == 4:
                        transpose_y(b, 7)
                        pe.wait_ge(y_lo.sem, y_lo.at(b, 16))
                    rope_product(b, j)
                pe.wait_ge(lx_added.sem, lx_added.at(b, NT))
                for i in range(NCTX // P):
                    last = product(ps[:, TILE_BANK[i // 2], D * (i % 2):D * (i % 2) + D],
                                   [(both(crT, slice(None), c, slice(P * i, P * i + P)), W("cv", c, 0, D)) for c in range(DC)])
                    if i % 2:
                        last.then_inc(lv_mm.sem, 1)
                attend(b, 1)

            def expert_hidden(b, e, par):
                for m in range(DC):
                    last = product(ps[:, 2 * par + m, :],
                                   [(tuple(ew[:, part, bass.ds(e * EW + D * c + P * m, P)] for part in range(2)),
                                     both(yT, slice(None), c)) for c in range(DC)])
                    last.then_inc(e_h.sem, 1)

            def expert_out(b, e, par):
                pe.wait_ge(e_split.sem, e_split.at(b, e + 1))
                for i in range(NT):
                    last = product(ps[:, 4 + 2 * par + i // 2, D * (i % 2):D * (i % 2) + D],
                                   [(both(hgT[par], slice(None), c, slice(P * i, P * i + P)),
                                     tuple(ew[:, part, bass.ds(e * EW + DC * D + D * c, D)] for part in range(2)))
                                    for c in range(DC)])
                last.then_inc(e_y.sem, 1)

            def routed(b):
                pe.wait_ge(var_ready.sem, var_ready.at(b, 9))
                keep_warm(10, 4)
                transpose_y(b, 9)
                keep_warm(6, 4)
                pe.wait_ge(y_lo.sem, y_lo.at(b, 20))
                for i in range(NT):
                    last = product(ps[:, 2, NE * i:NE * i + NE],
                                   [(both(yT, slice(None), c, slice(P * i, P * i + P)), W("g", c, 0, NE)) for c in range(DC)])
                last.then_inc(r_logits.sem, 1)
                pe.wait_ge(ew_in.sem, ew_in.at(b, 32))
                expert_hidden(b, 0, 0)
                pe.wait_ge(r_onehot.sem, r_onehot.at(b, 1))
                oh = lg[:, 5, :, :].bitcast(F16)
                for i in range(NT):
                    last = mm(ps[0:NE, 3, P * i:P * i + P], oh[:, i, 0:NE], ident16[:], start=True, stop=True)
                last.then_inc(r_oT.sem, 1)
                pe.wait_ge(r_mT.sem, r_mT.at(b, 1))
                for i in range(NT):
                    d_ = ps[:, 4 + i // 2, D * (i % 2):D * (i % 2) + D]
                    mm(d_, mT[0:NE, P * i:P * i + P], b2h[:], start=True, stop=False)
                    last = mm(d_, mT[0:NE, P * i:P * i + P], b2l[:], start=False, stop=True)
                last.then_inc(r_b2.sem, 1)
                with pe.Fori(0, NE // 2 - 1) as it:
                    for s_ in range(2):
                        expert_hidden(b, 2 * it + s_ + 1, 1 - s_)
                        expert_out(b, 2 * it + s_, s_)
                expert_hidden(b, NE - 1, 1)
                expert_out(b, NE - 2, 0)
                expert_out(b, NE - 1, 1)

            with pe.Fori(0, B) as b:
                windowed(b)
                latent(b)
                bitnet(b)
                self_attention(b)
                cross_attention(b)
                routed(b)

        @block.scalar
        def _(act):
            A = nc.scalar.activation
            act.sem_inc(lo_done.sem, 1)

            with act.Fori(0, WCH // 2) as it:
                for s_ in range(2):
                    act.wait_ge(w_in[s_].sem, 16 * it + 16)
                    A(wh[:, bass.ds((2 * it + s_) * WC, WC)], stage[:, s_, 0:WC], ACT.Copy).then_inc(w_hi.sem, 1)
            with act.Fori(0, 2) as it:
                for s_ in range(2):
                    act.wait_ge(w_in[s_].sem, 16 * (WCH // 2) + 16 * it + 16)
                    act.wait_ge(ew_out[s_].sem, ew_out[s_].at(0, 32 * it))
                    A(est[s_][0], stage[:, s_, :], ACT.Copy).then_inc(w_hi.sem, 1)
            act.wait_ge(const_in.sem, 16 * 8)
            A(b2h[:], b2[:], ACT.Copy).then_inc(w_hi.sem, 1)

            def load_table(slot, func):
                A(warm[:, slot:slot + 1], col[:, 0:1], func)

            def split_hi(b, k, dst, bias=None, aff_k=None):
                for c in range(DC):
                    if aff_k is not None:
                        act.wait_ge(aff_done.sem, aff_done.at(b, 2 * aff_k + c + 1))
                        A(dst[0][:, c, :], aff[:, c, :], ACT.Copy).then_inc(y_hi.sem, 1)
                        continue
                    act.wait_ge(y_t.sem, y_t.at(b, 2 * k + c + 1))
                    if bias:
                        A(dst[0][:, c, :], ps[:, c, :], ACT.Identity, bias=C(bias, c)).then_inc(y_hi.sem, 1)
                    else:
                        A(dst[0][:, c, :], ps[:, c, :], ACT.Copy).then_inc(y_hi.sem, 1)

            def windowed(b):
                load_table(0, ACT.Exp)
                split_hi(b, 0, yT)
                for j in range(7):
                    if j < 2:
                        act.wait_ge(a_q.sem, a_q.at(b, j + 1))
                        A(aqT[0][:, j, :], aff[:, j, :], ACT.Copy).then_inc(a_hi.sem, 1)
                        continue
                    act.wait_ge(a_proj.sem, a_proj.at(b, j + 1))
                    if j < 4:
                        A(akT[0][:, j - 2, :], ps[:, 2 + j, :], ACT.Identity, bias=C("abk", j - 2)).then_inc(a_hi.sem, 1)
                    elif j < 6:
                        A(av[0][:, 2 * (j - 4):2 * (j - 4) + 2, :].rearrange("p a n -> p (a n)"), ps[:, 2 + j, :], ACT.Copy)\
                            .then_inc(a_hi.sem, 1)
                    else:
                        A(av[0][:, NT, :], ps[:, 0, 0:D], ACT.Copy).then_inc(a_hi.sem, 1)
                act.wait_ge(a_max.sem, a_max.at(b, 1))
                for p_ in range(4):
                    last = A(a_p[:, p_, :], a_s[:, p_, :], ACT.Exp, bias=nm[:, p_:p_ + 1], accum_out=sums[:, p_:p_ + 1])
                last.then_inc(a_exp.sem, 1)
                split_hi(b, 1, CTX_DST[0], aff_k=0)
                act.wait_ge(a_pt.sem, a_pt.at(b, 1))
                A(a_pT[0].rearrange("p a n -> p (a n)"), banks(3, 2), ACT.Copy).then_inc(a_pthi.sem, 1)

            def unit_hi(b, h, par, k, n, bank=7):
                if k == 3:
                    act.wait_ge(u_q.sem, u_q.at(b, h + 1))
                    A(qT[par][0], rt_x, ACT.Copy).then_inc(u_hi.sem, 1)
                    return
                act.wait_ge(u_mm.sem, u_mm.at(b, n + 1))
                alone(act)
                if k < 3:
                    A(kT[par][0][:, 512 * k:512 * k + 512], ps[:, bank, :], ACT.Identity, bias=C("xbk", h)).then_inc(u_hi.sem, 1)
                elif k < 7:
                    A(v[par][0][:, 4 * (k - 4):4 * (k - 4) + 4, :].rearrange("p a n -> p (a n)"), ps[:, bank, :], ACT.Copy)\
                        .then_inc(u_hi.sem, 1)
                else:
                    A(oT[0][:, bass.ds(h, 1), :].rearrange("p a n -> p (a n)"), ps[:, bank, :], ACT.Identity,
                      bias=C("xbv", h)).then_inc(u_hi.sem, 1)

            def exps(b, n, i):
                act.wait_ge(s_max.sem, s_max.at(b, n + 1))
                A(xp, banks(0, 3), ACT.Exp, bias=nm[:, i:i + 1], accum_out=sums[:, i:i + 1]).then_inc(s_exp.sem, 1)

            def head(b, h, par, last_head):
                for i in range(NT):
                    n = h * NT + i
                    for g_ in range(3):
                        act.wait_ge(pt_mm.sem, pt_mm.at(b, 3 * n + g_ + 1))
                        A(xpT[0][:, 4 * g_:4 * g_ + 4, :].rearrange("p a n -> p (a n)"), ps[:, 3 + g_, :], ACT.Copy)\
                            .then_inc(pt_hi.sem, 1)
                    if not last_head:
                        unit_hi(b, h + 1, 1 - par, 2 * i, 7 + 8 * h + 2 * i)
                    if i < NT - 1 or not last_head:
                        exps(b, n + 1, (i + 1) % NT)
                    if i == NT - 1:
                        unit_hi(b, h, par, 7, 7 + 8 * h + (0 if last_head else 7))
                    elif not last_head:
                        unit_hi(b, h + 1, 1 - par, 2 * i + 1, 7 + 8 * h + 2 * i + 1)

            def latent(b):
                split_hi(b, 2, CTX_DST[1], aff_k=1)
                for n in range(2):
                    unit_hi(b, 0, 0, FIRST[n], n, FIRST_BANK[n])
                split_hi(b, 3, CTX_DST[2], aff_k=2)
                for n in range(2, 7):
                    unit_hi(b, 0, 0, FIRST[n], n, FIRST_BANK[n])
                exps(b, 0, 0)
                with act.Fori(0, XH // 2 - 1) as hp_:
                    for s_ in range(2):
                        head(b, 2 * hp_ + s_, s_, False)
                head(b, XH - 2, 0, False)
                head(b, XH - 1, 1, True)

            def bitnet(b):
                load_table(1, ACT.Silu)
                split_hi(b, 4, yT)

                def silu(m):
                    act.wait_ge(h_conv.sem, h_conv.at(b, m + 1))
                    A(g[:, m, :], conv[:, m % 2, 2, :], ACT.Silu).then_inc(h_silu.sem, 1)

                for m in range(NM):
                    act.wait_ge(h_mm.sem, h_mm.at(b, m + 1))
                    if m >= 3:
                        act.wait_ge(h_conv.sem, h_conv.at(b, m - 2))
                    A(hp[:, m % 3, 1:1 + S], ps[:, 2 + m % 2, :], ACT.Copy, scale=mw[:, 0:1]).then_inc(h_pad.sem, 1)
                    if m >= 2:
                        silu(m - 2)
                silu(NM - 2)
                silu(NM - 1)

                def scaled(i):
                    act.wait_ge(g_scale.sem, g_scale.at(b, i + 1))
                    A(gt[:, i % 2, :], banks(4 + 2 * (i % 2), 2), ACT.Identity, bias=C("round"),
                      scale=quant[:, 1, 2, i:i + 1]).then_inc(g_scaled.sem, 1)

                for i in range(3):
                    scaled(i)
                for j in range(NT):
                    act.wait_ge(gq_t.sem, gq_t.at(b, j + 1))
                    A(gq[:, :, P * j:P * j + P], ps[:, j % 2, :].bitcast(F16).rearrange("p (m n) -> p m n", m=NM), ACT.Copy)\
                        .then_inc(gq_done.sem, 1)
                    if j + 3 < NT:
                        scaled(j + 3)

            def values_hi(b, n, t, bank):
                act.wait_ge(lv_mm.sem, lv_mm.at(b, n + 1))
                A(v16[:, 2 * t:2 * t + 2, :, 1:1 + LD], ps[:, bank, :].rearrange("p (t h d) -> p t h d", t=2, d=LD), ACT.Copy)\
                    .then_inc(lv_hi.sem, 1)

            def unit_exp(b, mode, it, k, ahead=0):
                kk = k + ahead
                it, kk = it + kk // 4, kk % 4
                u = mode["first"] + it * 4 + kk
                act.wait_ge(ls_max.sem, ls_max.at(b, u + 1))
                if mode["heads"] == 2:
                    for t in range(2):
                        last = A(lp[:, kk % 2, 512 * t:512 * t + 512], ps[:, 2 * (kk % 2) + t, :], ACT.Exp,
                                 bias=nm[:, 2 * kk + t:2 * kk + t + 1])
                else:
                    last = A(lp[:, kk % 2, :], banks(2 * (kk % 2), 2), ACT.Exp, bias=nm[:, 2 * kk:2 * kk + 1])
                last.then_inc(ls_exp.sem, 1)

            def unit_hi_l(b, mode, it, k, more):
                u = mode["first"] + it * 4 + k
                if more:
                    unit_exp(b, mode, it, k, 1)
                for g_ in range(2):
                    act.wait_ge(lt_mm.sem, lt_mm.at(b, 2 * u + g_ + 1))
                    A(lpT[k % 2][0][:, 4 * g_:4 * g_ + 4, :].rearrange("p a n -> p (a n)"), ps[:, 4 + g_, :], ACT.Copy)\
                        .then_inc(lt_hi.sem, 1)

            def body_out(b, mode, it):
                act.wait_ge(lo_mm.sem, lo_mm.at(b, mode["first"] + it * 4 + 4))
                alone(act)
                hb = mode["heads"]
                src = ps[:, 6, 0:NT * hb * VW].rearrange("p (t h n) -> p t h n", t=NT, h=hb)
                A(os_[:, :, bass.ds(it * hb, hb), 0:VW - 1], src[:, :, :, 0:VW - 1], ACT.Copy).then_inc(lo_done.sem, 1)

            def attend(b, m_):
                mode = MODES[m_]
                nb = mode["bodies"]
                for sent in (k_out, q_out):
                    act.wait_ge(sent.sem, sent.at(b, 64 * (m_ + 1)))
                unit_exp(b, mode, 0, 0)
                for k in range(4):
                    unit_hi_l(b, mode, 0, k, True)
                with act.Fori(1, nb - 1) as it:
                    for k in range(4):
                        unit_hi_l(b, mode, it, k, True)
                        if k == 0:
                            body_out(b, mode, it - 1)
                for k in range(4):
                    unit_hi_l(b, mode, nb - 1, k, k < 3)
                    if k == 0:
                        body_out(b, mode, nb - 2)
                body_out(b, mode, nb - 1)
                split_hi(b, 6 + 2 * m_, yT, bias=("sbv", "cbv")[m_])
                if m_ == 0:
                    for j in range(2):
                        rotated_hi(b, j)

            def rotated_hi(b, j):
                act.wait_ge(rp_sum.sem, rp_sum.at(b, j + 1))
                t0 = 512 * (j % 2)
                dst = dq[0][:, j - 4, :] if j >= 4 else dk[0][:, j // 2, t0:t0 + 512]
                A(dst, rt[:, j % 2, 0, :], ACT.Copy).then_inc(rp_hi.sem, 1)

            def self_attention(b):
                load_table(2, ACT.Exp)
                split_hi(b, 5, yT)
                for c in range(DC):
                    act.wait_ge(lq_mm.sem, lq_mm.at(b, 2 * c + 1))
                    A(dk[0][:, c, 0:S], ps[:, 2 + 2 * c, :], ACT.Identity, bias=C("sbk", c)).then_inc(lq_hi.sem, 1)
                    act.wait_ge(lq_q.sem, lq_q.at(b, c + 1))
                    A(dq[0][:, c, :], rt[:, 0, c, :], ACT.Copy).then_inc(lq_hi.sem, 1)
                act.wait_ge(ones_set.sem, ones_set.at(b, 1))
                for t in range(2):
                    values_hi(b, t, t, 6 + t)
                act.wait_ge(craw_in.sem, craw_in.at(b, 16))
                for c in range(DC):
                    A(crT[0][:, c, :], craw[:, c, :], ACT.Copy).then_inc(cr_hi.sem, 1)
                attend(b, 0)

            def cross_attention(b):
                split_hi(b, 7, yT)
                for j in range(2, 6):
                    rotated_hi(b, j)
                for t in range(4):
                    values_hi(b, 2 + t, t, TILE_BANK[t])
                attend(b, 1)

            def routed(b):
                load_table(3, ACT.Gelu)
                split_hi(b, 9, yT)
                act.wait_ge(r_oT.sem, r_oT.at(b, 1))
                A(mT[0:NE, :], ps[0:NE, 3, :], ACT.Copy).then_inc(r_mT.sem, 1)
                with act.Fori(0, NE // 2) as it:
                    for s_ in range(2):
                        act.wait_ge(e_split.sem, e_split.at(b, 2 * it))
                        for m in range(DC):
                            act.wait_ge(e_h.sem, e_h.at(b, 4 * it + 2 * s_ + m + 1))
                            alone(act)
                            A(hg[:, s_, m, :], ps[:, 2 * s_ + m, :], ACT.Gelu,
                              bias=C("b1", (2 * it + s_) * DC + m)).then_inc(e_gelu.sem, 1)

            with act.Fori(0, B) as b:
                windowed(b)
                latent(b)
                bitnet(b)
                self_attention(b)
                cross_attention(b)
                routed(b)

        @block.vector
        def _(dve):
            V = nc.vector
            own = Order(dve, dve_own.sem)
            TT, TS_, STT = V.tensor_tensor, V.tensor_scalar, V.scalar_tensor_tensor

            for signal in (w_lo, u_lo, o_done, e_added, e_split, rp_lo):
                dve.sem_inc(signal.sem, 1)
            for k in range(2):
                dve.wait_ge(t_in.sem, 32)
                V.tensor_reduce(wsum[:, k:k + 1], tstage[k], AX.X, ALU.add, apply_absolute_value=True).then_inc(t_sum.sem, 1)
            with dve.Fori(0, WCH // 2) as it:
                for s_ in range(2):
                    dve.wait_ge(w_hi.sem, 2 * it + s_ + 1)
                    at = bass.ds((2 * it + s_) * WC, WC)
                    TT(wl[:, at], stage[:, s_, 0:WC], wh[:, at], ALU.subtract).then_inc(w_lo.sem, 1)
            with dve.Fori(0, 2) as it:
                for s_ in range(2):
                    dve.wait_ge(w_hi.sem, WCH + 2 * it + s_ + 1)
                    TT(est[s_][1], stage[:, s_, :], est[s_][0], ALU.subtract).then_inc(w_lo.sem, 1)
            dve.wait_ge(t_all.sem, 1)
            own.link(TS_(mw[:], ps[:, 0, 0:2], 1.0 / (D * HID), 1e-5, ALU.mult, ALU.max))
            own.link(V.reciprocal(msc[:], mw[:]))
            for k in range(2):
                own.link(TS_(tstage[k], tstage[k], msc[:, k:k + 1], ROUND, ALU.mult, ALU.add))
                own.link(TS_(tstage[k], tstage[k], ROUND, -1.0, ALU.subtract, ALU.max))
                TS_(tern[:, k, :], tstage[k], 1.0, None, ALU.min).then_inc(t_done.sem, 1)
            dve.wait_ge(w_hi.sem, WCH + 5)
            own.link(TT(b2l[:], b2[:], b2h[:], ALU.subtract))
            dve.wait_ge(const_in.sem, 16 * 8)

            def stats(src, i):
                own.mark(V.bn_stats(st[:, i, :], src[:, i, :]))

            def moments(b, k, src, first=0):
                for i in range(first, NT):
                    stats(src, i)
                own.wait()
                alone(dve)
                for i in range(NT):
                    own.mark(V.bn_aggr(mv[:, i, :], st[:, i, :]))
                own.wait()
                TS_(ve[:], mv[:, :, 1], 1e-5, None, ALU.add).then_inc(var_ready.sem, 1)

            def normalise(b, k, src, dst):
                dve.wait_ge(rstd_ready.sem, rstd_ready.at(b, k + 1))
                for i in range(NT):
                    last = TS_(dst[:, i, :], src[:, i, :], mv[:, i, 0:1], rstd[:, i:i + 1], ALU.subtract, ALU.mult)
                return last

            def norm(b, k, src, dst, first=0):
                moments(b, k, src, first)
                return normalise(b, k, src, dst)

            def affine(b, k, aff_k, at=(0, 1)):
                gn, bn = (("gm", "bm"), ("gm", "bm"), ("gl", "bl"))[aff_k]
                for c in range(DC):
                    dve.wait_ge(y_t.sem, y_t.at(b, 2 * k + c + 1))
                    TS_(aff[:, c, :], ps[:, at[c], :], C(gn, c), C(bn, c), ALU.mult, ALU.add).then_inc(aff_done.sem, 1)

            def split_lo(b, k, dst, bias=None, aff_k=None):
                for c in range(DC):
                    dve.wait_ge(y_hi.sem, y_hi.at(b, 2 * k + c + 1))
                    if aff_k is not None:
                        ins = TT(dst[1][:, c, :], aff[:, c, :], dst[0][:, c, :], ALU.subtract)
                    elif bias:
                        ins = STT(dst[1][:, c, :], ps[:, c, :], C(bias, c), dst[0][:, c, :], ALU.add, ALU.subtract)
                    else:
                        ins = TT(dst[1][:, c, :], ps[:, c, :], dst[0][:, c, :], ALU.subtract)
                    ins.then_inc(y_lo.sem, 1)

            def add_rows(bias):
                own.link(TT(x[:], x[:], rows4(R(bias)), ALU.add))

            def windowed(b):
                dve.wait_ge(y_in.sem, y_in.at(b, 16))
                norm(b, 0, y, y).then_inc(y_ready.sem, 1)
                split_lo(b, 0, yT)
                dve.wait_ge(ctx_in_s.sem, ctx_in_s.at(b, 16))
                moments(b, 1, ctx_tok[:, 0:NT, :])
                for j in range(2):
                    dve.wait_ge(a_proj.sem, a_proj.at(b, j + 1))
                    TS_(aff[:, j, :], ps[:, 2 + j, :], C("abq", j), float(D) ** -0.5, ALU.add, ALU.mult).then_inc(a_q.sem, 1)
                normalise(b, 1, ctx_tok[:, 0:NT, :], y).then_inc(y_ready.sem, 1)
                for j in range(7):
                    dve.wait_ge(a_hi.sem, a_hi.at(b, j + 1))
                    if j < 2:
                        ins = TT(aqT[1][:, j, :], aff[:, j, :], aqT[0][:, j, :], ALU.subtract)
                    elif j < 4:
                        ins = STT(akT[1][:, j - 2, :], ps[:, 2 + j, :], C("abk", j - 2), akT[0][:, j - 2, :], ALU.add, ALU.subtract)
                    elif j < 6:
                        t0 = 2 * (j - 4)
                        ins = TT(av[1][:, t0:t0 + 2, :].rearrange("p a n -> p (a n)"), ps[:, 2 + j, :],
                                 av[0][:, t0:t0 + 2, :].rearrange("p a n -> p (a n)"), ALU.subtract)
                    else:
                        ins = TT(av[1][:, NT, :], ps[:, 0, 0:D], av[0][:, NT, :], ALU.subtract)
                    ins.then_inc(a_lo.sem, 1)
                dve.wait_ge(x_in.sem, x_in.at(b, 16))
                add_rows("abv")
                dve.wait_ge(a_scores.sem, a_scores.at(b, 1))
                own.link(TT(a_s, banks(1, 2).rearrange("p (a n) -> p a n", a=4), mask[:], ALU.add))
                V.tensor_reduce(nm[:, 0:4], a_s, AX.X, ALU.max, negate=True).then_inc(a_max.sem, 1)
                affine(b, 1, 0, CTX_AT)
                moments(b, 2, ctx_tok[:, NT:2 * NT, :])
                dve.wait_ge(a_exp.sem, a_exp.at(b, 1))
                own.link(V.reciprocal(rs[:], sums[:]))
                split_lo(b, 1, CTX_DST[0], aff_k=0)
                dve.wait_ge(a_pthi.sem, a_pthi.at(b, 1))
                TT(a_pT[1].rearrange("p a n -> p (a n)"), banks(3, 2), a_pT[0].rearrange("p a n -> p (a n)"), ALU.subtract)\
                    .then_inc(a_ptlo.sem, 1)
                normalise(b, 2, ctx_tok[:, NT:2 * NT, :], y).then_inc(y_ready.sem, 1)
                dve.wait_ge(a_out.sem, a_out.at(b, 1))
                for i in range(NT):
                    own.mark(STT(x[:, i, :], ps[:, 5 + i // 2, D * (i % 2):D * (i % 2) + D], rs[:, i:i + 1], x[:, i, :],
                                 ALU.mult, ALU.add))
                own.wait()

            def unit_lo(b, h, par, k, n, bank=7):
                if k == 3:
                    dve.wait_ge(u_mm.sem, u_mm.at(b, n + 1))
                    TS_(rt_x, ps[:, bank, :], C("xbq", h), XS, ALU.add, ALU.mult).then_inc(u_q.sem, 1)
                dve.wait_ge(u_hi.sem, u_hi.at(b, n + 1))
                if k < 3:
                    sl = slice(512 * k, 512 * k + 512)
                    ins = STT(kT[par][1][:, sl], ps[:, bank, :], C("xbk", h), kT[par][0][:, sl], ALU.add, ALU.subtract)
                elif k == 3:
                    ins = TT(qT[par][1], rt_x, qT[par][0], ALU.subtract)
                elif k < 7:
                    sl = slice(4 * (k - 4), 4 * (k - 4) + 4)
                    ins = TT(v[par][1][:, sl, :].rearrange("p a n -> p (a n)"), ps[:, bank, :],
                             v[par][0][:, sl, :].rearrange("p a n -> p (a n)"), ALU.subtract)
                else:
                    ins = STT(oT[1][:, bass.ds(h, 1), :].rearrange("p a n -> p (a n)"), ps[:, bank, :], C("xbv", h),
                              oT[0][:, bass.ds(h, 1), :].rearrange("p a n -> p (a n)"), ALU.add, ALU.subtract)
                ins.then_inc(u_lo.sem, 1)

            def maxes(b, n, i):
                dve.wait_ge(s_mm.sem, s_mm.at(b, n + 1))
                V.tensor_reduce(nm[:, i:i + 1], banks(0, 3), AX.X, ALU.max, negate=True).then_inc(s_max.sem, 1)

            def head(b, h, par, last_head):
                for i in range(NT):
                    n = h * NT + i
                    for g_ in range(3):
                        dve.wait_ge(pt_hi.sem, pt_hi.at(b, 3 * n + g_ + 1))
                        sl = slice(4 * g_, 4 * g_ + 4)
                        TT(xpT[1][:, sl, :].rearrange("p a n -> p (a n)"), ps[:, 3 + g_, :],
                           xpT[0][:, sl, :].rearrange("p a n -> p (a n)"), ALU.subtract).then_inc(pt_lo.sem, 1)
                    own.mark(V.reciprocal(rs[:, i:i + 1], sums[:, i:i + 1]))
                    if i < NT - 1 or not last_head:
                        maxes(b, n + 1, (i + 1) % NT)
                    if not last_head:
                        unit_lo(b, h + 1, 1 - par, 2 * i, 7 + 8 * h + 2 * i)
                    own.wait()
                    dve.wait_ge(o_mm.sem, o_mm.at(b, n + 1))
                    TS_(on[:, i, :], ps[:, 6, P * i:P * i + P], rs[:, i:i + 1], None, ALU.mult).then_inc(o_done.sem, 1)
                    if i == NT - 1:
                        unit_lo(b, h, par, 7, 7 + 8 * h + (0 if last_head else 7))
                    elif not last_head:
                        unit_lo(b, h + 1, 1 - par, 2 * i + 1, 7 + 8 * h + 2 * i + 1)

            def latent(b):
                moments(b, 3, x)
                affine(b, 2, 1, CTX_AT)
                own.link(normalise(b, 3, x, lat))
                moments(b, 4, lat)
                split_lo(b, 2, CTX_DST[1], aff_k=1)
                normalise(b, 4, lat, y).then_inc(y_ready.sem, 1)
                for n in range(2):
                    unit_lo(b, 0, 0, FIRST[n], n, FIRST_BANK[n])
                affine(b, 3, 2)
                split_lo(b, 3, CTX_DST[2], aff_k=2)
                for n in range(2, 7):
                    unit_lo(b, 0, 0, FIRST[n], n, FIRST_BANK[n])
                maxes(b, 0, 0)
                with dve.Fori(0, XH // 2 - 1) as hp_:
                    own.enter(hp_, 0, 2 * NT)
                    for s_ in range(2):
                        head(b, 2 * hp_ + s_, s_, False)
                    own.leave(XH // 2 - 1)
                head(b, XH - 2, 0, False)
                head(b, XH - 1, 1, True)
                add_rows("xbo")
                dve.wait_ge(xo_mm.sem, xo_mm.at(b, 1))
                TT(x[:], ps[:, 0:NT, 0:D], x[:], ALU.add).then_inc(xo_added.sem, 1)
                dve.wait_ge(xo_added.sem, xo_added.at(b, 1))

            def scales(slots, src, scale_of_w=None, ready=None):
                am, ri, sc, iv = (slots[:, r] for r in range(4))
                own.link(V.tensor_reduce(am, src, AX.X, ALU.max, apply_absolute_value=True))
                own.link(TS_(am, am, 1e-5, None, ALU.max))
                own.link(V.reciprocal(ri, am))
                ins = TS_(sc, ri, 127.0, None, ALU.mult)
                if ready:
                    ins.then_inc(ready.sem, 1)
                else:
                    own.mark(ins)
                if scale_of_w is None:
                    own.mark(TS_(iv, am, 1.0 / 127.0, None, ALU.mult))
                else:
                    own.mark(TS_(iv, am, 1.0 / 127.0, scale_of_w, ALU.mult, ALU.mult))
                own.wait()
                return (sc, iv) if ready is None else iv

            def bitnet(b):
                own.link(norm(b, 5, x, y))
                sc, iv = scales(quant[:, 0], y[:])
                for i in range(NT):
                    own.mark(TS_(y[:, i, :], y[:, i, :], sc[:, i:i + 1], ROUND, ALU.mult, ALU.add))
                own.wait()
                own.link(TS_(y[:], y[:], ROUND, 127.0, ALU.subtract, ALU.min))
                for i in range(NT):
                    last = TS_(y[:, i, :], y[:, i, :], -128.0, iv[:, i:i + 1], ALU.max, ALU.mult)
                last.then_inc(y_ready.sem, 1)
                split_lo(b, 4, yT)
                for k in range(3):
                    own.mark(V.memset(hp[:, k, 0:1], 0.0))
                    own.mark(V.memset(hp[:, k, 1 + S:2 + S], 0.0))
                own.wait()

                def tap(m, k):
                    src, dst = hp[:, m % 3, k:k + S], conv[:, m % 2, k, :]
                    if k == 0:
                        dve.wait_ge(h_pad.sem, h_pad.at(b, m + 1))
                        own.mark(TS_(dst, src, C("cw", 3 * m), C("cb", m), ALU.mult, ALU.add))
                        return
                    ins = STT(dst, src, C("cw", 3 * m + k), conv[:, m % 2, k - 1, :], ALU.mult, ALU.add)
                    if k == 1:
                        own.mark(ins)
                    else:
                        ins.then_inc(h_conv.sem, 1)

                for m in range(-1, NM + 1):
                    if m >= 1:
                        if m >= 3:
                            dve.wait_ge(h_silu.sem, h_silu.at(b, m - 2))
                        own.wait(1 if m < NM else 0)
                        tap(m - 1, 2)
                    if 0 <= m < NM:
                        own.wait()
                        tap(m, 1)
                    if m + 1 < NM:
                        if m >= 1:
                            dve.wait_ge(h_conv.sem, h_conv.at(b, m))
                        tap(m + 1, 0)

                def row_scales(i):
                    dve.wait_ge(g_t.sem, g_t.at(b, i + 1))
                    return scales(quant[:, 1, :, i:i + 1], banks(4 + 2 * (i % 2), 2).unsqueeze(1), mw[:, 1:2], g_scale)

                def quantise(i):
                    q = i % 2
                    dve.wait_ge(g_scaled.sem, g_scaled.at(b, i + 1))
                    own.mark(TS_(gt[:, q, :], gt[:, q, :], ROUND, -128.0, ALU.subtract, ALU.max))
                    if i >= 2:
                        dve.wait_ge(gq_t.sem, gq_t.at(b, i - 1))
                    own.wait()
                    TS_(gi[:, q, :], gt[:, q, :], 127.0, None, ALU.min).then_inc(g_quant.sem, 1)

                def add_tile(j, iv):
                    dve.wait_ge(f_mm.sem, f_mm.at(b, j + 1))
                    STT(x[:, j, :], ps[:, 2 + j % 2, 0:D], iv, x[:, j, :], ALU.mult, ALU.add).then_inc(f_added.sem, 1)

                ivs = [row_scales(0), row_scales(1)]
                for i in range(2, NT):
                    quantise(i - 2)
                    ivs.append(row_scales(i))
                quantise(NT - 2)
                add_tile(0, ivs[0])
                quantise(NT - 1)
                for j in range(1, NT + 1):
                    if j < NT:
                        add_tile(j, ivs[j])
                    dve.wait_ge(f_added.sem, f_added.at(b, j))
                    stats(x, j - 1)

            def values_lo(b, n, t, bank):
                dve.wait_ge(lv_hi.sem, lv_hi.at(b, n + 1))
                TT(v16[:, 2 * t:2 * t + 2, :, 1 + LD:1 + 2 * LD], ps[:, bank, :].rearrange("p (t h d) -> p t h d", t=2, d=LD),
                   v16[:, 2 * t:2 * t + 2, :, 1:1 + LD], ALU.subtract).then_inc(lv_lo.sem, 1)

            def unit_max(b, mode, it, k, ahead=0):
                kk = k + ahead
                it, kk = it + kk // 4, kk % 4
                u = mode["first"] + it * 4 + kk
                dve.wait_ge(ls_mm.sem, ls_mm.at(b, u + 1))
                src = banks(2 * (kk % 2), 2)
                if mode["heads"] == 2:
                    src = src.rearrange("p (t n) -> p t n", t=2)
                V.tensor_reduce(nm[:, 2 * kk:2 * kk + mode["heads"]], src, AX.X, ALU.max, negate=True).then_inc(ls_max.sem, 1)

            def unit_lo_l(b, mode, it, k, more):
                u = mode["first"] + it * 4 + k
                if more:
                    unit_max(b, mode, it, k, 2)
                for g_ in range(2):
                    dve.wait_ge(lt_hi.sem, lt_hi.at(b, 2 * u + g_ + 1))
                    sl = slice(4 * g_, 4 * g_ + 4)
                    TT(lpT[k % 2][1][:, sl, :].rearrange("p a n -> p (a n)"), ps[:, 4 + g_, :],
                       lpT[k % 2][0][:, sl, :].rearrange("p a n -> p (a n)"), ALU.subtract).then_inc(lt_lo.sem, 1)

            def rotate(b, j):
                dve.wait_ge(rp_mm.sem, rp_mm.at(b, j + 1))
                if j >= 2:
                    dve.wait_ge(rp_lo.sem, rp_lo.at(b, j - 1))
                m = j - 4 if j >= 4 else j // 2
                t0 = 512 * (j % 2)
                tab = rope_q if j >= 4 else rope_k[:, :, t0:t0 + 512]
                names = ("cbq", "cbqs") if j >= 4 else ("cbk", "cbks")
                r_ = rt[:, j % 2]
                for s_ in range(2):
                    last = STT(r_[:, s_, :], ps[:, 4 + 2 * (j % 2) + s_, :], C(names[s_], m), tab[:, s_, :], ALU.add, ALU.mult)
                last.then_inc(rp_mul.sem, 1)
                if j >= 4:
                    dve.wait_ge(rp_mul.sem, rp_mul.at(b, j + 1))
                    dve.wait_ge(rp_sum.sem, rp_sum.at(b, j))
                    TT(r_[:, 0, :], r_[:, 0, :], r_[:, 1, :], ALU.add).then_inc(rp_sum.sem, 1)

            def rotated_lo(b, j):
                dve.wait_ge(rp_hi.sem, rp_hi.at(b, j + 1))
                t0 = 512 * (j % 2)
                hi, lo = (t[:, j - 4, :] if j >= 4 else t[:, j // 2, t0:t0 + 512] for t in (dq if j >= 4 else dk))
                TT(lo, rt[:, j % 2, 0, :], hi, ALU.subtract).then_inc(rp_lo.sem, 1)

            def attend(b, m_):
                mode = MODES[m_]
                nb = mode["bodies"]
                for u in range(2):
                    unit_max(b, mode, 0, u)
                with dve.Fori(0, nb - 1) as it:
                    for k in range(4):
                        unit_lo_l(b, mode, it, k, True)
                for k in range(4):
                    unit_lo_l(b, mode, nb - 1, k, k < 2)
                dve.wait_ge(lo_done.sem, lo_done.at(b, mode["body0"] + nb))
                own.mark(V.reciprocal(rl[:].rearrange("p (t h) -> p t h", t=NT), os_[:, :, :, 0]))
                yv = y[:].rearrange("p t (h d) -> p t h d", d=LD)
                rv = rl[:].rearrange("p (t h) -> p t h", t=NT).unsqueeze(3).to_broadcast([P, NT, LH, LD])
                for c, done in enumerate((y_half, y_ready)):
                    hs = slice(P // LD * c, P // LD * (c + 1))
                    own.link(TT(yv[:, :, hs], os_[:, :, hs, 1:1 + LD], os_[:, :, hs, 1 + LD:1 + 2 * LD], ALU.add))
                    TT(yv[:, :, hs], yv[:, :, hs], rv[:, :, hs], ALU.mult).then_inc(done.sem, 1)
                split_lo(b, 6 + 2 * m_, yT, bias=("sbv", "cbv")[m_])
                add_rows(("sbo", "cbo")[m_])
                if m_ == 0:
                    rotate(b, 0)
                for i in range(NT + 1):
                    if i < NT:
                        dve.wait_ge(lx_mm.sem, lx_mm.at(b, NT * m_ + i + 1))
                        TT(x[:, i, :], ps[:, TILE_BANK[i], 0:D], x[:, i, :], ALU.add).then_inc(lx_added.sem, 1)
                    if i >= 1:
                        dve.wait_ge(lx_added.sem, lx_added.at(b, NT * m_ + i))
                        stats(x, i - 1)

            def self_attention(b):
                norm(b, 6, x, y, NT).then_inc(y_ready.sem, 1)
                split_lo(b, 5, yT)
                V.memset(v16[:, :, :, 0:1], 1.0).then_inc(ones_set.sem, 1)
                for c in range(DC):
                    dve.wait_ge(lq_hi.sem, lq_hi.at(b, 2 * c + 1))
                    STT(dk[1][:, c, 0:S], ps[:, 2 + 2 * c, :], C("sbk", c), dk[0][:, c, 0:S], ALU.add, ALU.subtract)\
                        .then_inc(lq_lo.sem, 1)
                    dve.wait_ge(lq_mm.sem, lq_mm.at(b, 2 * c + 2))
                    TS_(rt[:, 0, c, :], ps[:, 3 + 2 * c, :], C("sbq", c), LD ** -0.5, ALU.add, ALU.mult).then_inc(lq_q.sem, 1)
                    dve.wait_ge(lq_hi.sem, lq_hi.at(b, 2 * c + 2))
                    TT(dq[1][:, c, :], rt[:, 0, c, :], dq[0][:, c, :], ALU.subtract).then_inc(lq_lo.sem, 1)
                for t in range(2):
                    values_lo(b, t, t, 6 + t)
                for c in range(DC):
                    dve.wait_ge(cr_hi.sem, cr_hi.at(b, c + 1))
                    TT(crT[1][:, c, :], craw[:, c, :], crT[0][:, c, :], ALU.subtract).then_inc(cr_lo.sem, 1)
                attend(b, 0)

            def cross_attention(b):
                moments(b, 7, x, NT)
                rotate(b, 1)
                rotated_lo(b, 0)
                normalise(b, 7, x, y).then_inc(y_ready.sem, 1)
                rotated_lo(b, 1)
                rotate(b, 2)
                split_lo(b, 7, yT)
                for j in range(3, 5):
                    rotate(b, j)
                    rotated_lo(b, j - 1)
                rotated_lo(b, 4)
                rotate(b, 5)
                rotated_lo(b, 5)
                for t in range(4):
                    values_lo(b, 2 + t, t, TILE_BANK[t])
                attend(b, 1)

            def split_hidden(b, e, par):
                dve.wait_ge(e_gelu.sem, e_gelu.at(b, 2 * e + 2))
                own.link(V.tensor_copy(hgT[par][0], hg[:, par, :, :]))
                TT(hgT[par][1], hg[:, par, :, :], hgT[par][0], ALU.subtract).then_inc(e_split.sem, 1)

            def add_expert(b, e, par):
                dve.wait_ge(e_y.sem, e_y.at(b, e + 1))
                for i in range(NT):
                    last = STT(x[:, i, :], ps[:, 4 + 2 * par + i // 2, D * (i % 2):D * (i % 2) + D],
                               lg[:, 4, i, bass.ds(e, 1)], x[:, i, :], ALU.mult, ALU.add)
                last.then_inc(e_added.sem, 1)
                dve.wait_ge(e_added.sem, e_added.at(b, e + 1))

            def routed(b):
                norm(b, 8, x, y, NT).then_inc(y_ready.sem, 1)
                split_lo(b, 9, yT)
                dve.wait_ge(r_logits.sem, r_logits.at(b, 1))
                own.link(TT(lg[:, 0], ps[:, 2, 0:NT * NE].rearrange("p (t e) -> p t e", t=NT), rows4(R("bg", NE)), ALU.add))
                own.link(V.tensor_reduce(lg[:, 1, :, 0], lg[:, 0], AX.X, ALU.max))
                own.link(TT(lg[:, 2], lg[:, 0], lg[:, 1, :, 0:1].to_broadcast([P, NT, NE]), ALU.is_ge))
                own.link(TT(lg[:, 3], lg[:, 2], rows4(R("order", NE)), ALU.mult))
                own.link(V.tensor_reduce(lg[:, 1, :, 1], lg[:, 3], AX.X, ALU.max))
                own.link(TT(lg[:, 4], lg[:, 3], lg[:, 1, :, 1:2].to_broadcast([P, NT, NE]), ALU.is_equal))
                V.tensor_copy(lg[:, 5, :, :].bitcast(F16)[:, :, 0:NE], lg[:, 4]).then_inc(r_onehot.sem, 1)
                dve.wait_ge(r_b2.sem, r_b2.at(b, 1))
                own.link(TT(x[:], banks(4, 2).rearrange("p (a n) -> p a n", a=NT), x[:], ALU.add))
                split_hidden(b, 0, 0)
                with dve.Fori(0, NE // 2 - 1) as it:
                    own.enter(it, 0, 2)
                    for s_ in range(2):
                        split_hidden(b, 2 * it + s_ + 1, 1 - s_)
                        add_expert(b, 2 * it + s_, s_)
                    own.leave(NE // 2 - 1)
                split_hidden(b, NE - 1, 1)
                add_expert(b, NE - 2, 0)
                add_expert(b, NE - 1, 1)

            with dve.Fori(0, B) as b:
                own.enter(b, 0, OWN_PER_BATCH)
                windowed(b)
                latent(b)
                bitnet(b)
                self_attention(b)
                cross_attention(b)
                routed(b)
                own.leave(B)


def chunks(w):
    k, n = w.shape
    return w.reshape(k // P, P, n).transpose(1, 0, 2).reshape(P, -1)


def columns(v_):
    return v_.reshape(-1, P).T


def swap_halves(w):
    s = w.shape
    return w.reshape(s[:-1] + (LH, 2, LD // 2))[..., ::-1, :].reshape(s)


def window_mask():
    q, c = np.arange(P)[:, None], np.arange(2 * P)[None, :]
    near = (c // BL >= q // BL) & (c // BL <= q // BL + 2)
    m = np.zeros((P, 4, 2 * P), np.float32)
    for p_ in range(4):
        token = P * p_ - BL + c
        m[:, p_, :] = np.where(near & (token >= 0) & (token < S), 0.0, -1e30)
    return m


def rope_table(n, scale):
    inv = np.float32(1.0) / np.float32(10000.0) ** (np.arange(0, LD, 2, dtype=np.float32) / np.float32(LD))
    t = np.arange(n, dtype=np.float32)
    f = np.outer(np.float32(10.0) * (t / np.float32(n)), inv).astype(np.float32)
    cos, sin = np.cos(f).T, np.sin(f).T
    c = np.tile(np.concatenate([cos, cos]), (P // LD, 1))
    s = np.tile(np.concatenate([-sin, sin]), (P // LD, 1))
    return (np.stack([c, s], 1) * scale).astype(np.float32)


def kernel(**inputs):
    import concourse.bacc as bacc
    from concourse.bass_utils import run_bass_kernel_spmd

    i = {k: np.asarray(v_) for k, v_ in inputs.items()}
    names = dict(aq="L0_attn_Wq", ak="L0_attn_Wk", av="L0_attn_Wv", xq="L0_xattn_Wq", xkv="L0_xattn_Wkv",
                 xo="L0_xattn_Wo", g="L1_ffn_Wg")
    names_t = dict(sq="L1_attn_Wq", sk="L1_attn_Wk", sv="L1_attn_Wv", so="L1_attn_Wo", cq="L1_xattn_Wq",
                   ck="L1_xattn_Wk", cv="L1_xattn_Wv", co="L1_xattn_Wo")
    w = {k: i[n] for k, n in names.items()}
    w |= {k: i[n].T for k, n in names_t.items()}
    w["cqs"], w["cks"] = swap_halves(w["cq"]), swap_halves(w["ck"])
    weights = np.concatenate([chunks(w[k]) for k, _, _ in RESIDENT], 1)
    experts = np.concatenate([chunks(i[n][e]) for e in range(NE) for n in ("L1_ffn_W1", "L1_ffn_W2")], 1)
    ternary = np.stack([chunks(i["L0_ffn_w1"].T), chunks(i["L0_ffn_w2"].T)])
    bkv = i["L0_xattn_bkv"]
    cbq, cbk = i["L1_xattn_bq"], i["L1_xattn_bk"]
    cw = i["L0_ffn_conv_w"][:, 0, :].reshape(NM, P, 3).transpose(1, 0, 2).reshape(P, -1)
    cols = [columns(i["L0_attn_bq"]), columns(i["L0_attn_bk"]), columns(i["L0_xattn_bq"]), columns(bkv[:XIN]),
            columns(bkv[XIN:]), columns(i["L0_xattn_gamma_media"]), columns(i["L0_xattn_beta_media"]),
            columns(i["L0_xattn_gamma_lat"]), columns(i["L0_xattn_beta_lat"]), cw, columns(i["L0_ffn_conv_b"]),
            columns(i["L1_attn_bq"]), columns(i["L1_attn_bk"]), columns(i["L1_attn_bv"]), columns(cbq),
            columns(swap_halves(cbq)), columns(cbk), columns(swap_halves(cbk)), columns(i["L1_xattn_bv"]),
            columns(i["L1_ffn_b1"].reshape(-1)), np.full((P, 4), -0.5, np.float32), np.full((P, 1), ROUND, np.float32)]
    rows = np.concatenate([i["L0_attn_bv"], i["L0_xattn_bo"], i["L1_attn_bo"], i["L1_xattn_bo"], i["L1_ffn_bg"],
                           np.arange(NE, 0, -1, dtype=np.float32)])
    arrays = {
        "x": i["x"], "ctx": i["ctx_1024"], "ctx_t": i["ctx_1024"].transpose(0, 2, 1), "weights": weights,
        "experts": experts, "ternary": ternary, "cols": np.concatenate(cols, 1),
        "rows": np.broadcast_to(rows, (P, NROW)), "b2": i["L1_ffn_b2"], "window": window_mask(),
        "rope_q": rope_table(S, LD ** -0.5), "rope_k": rope_table(NCTX, 1.0),
        "eye": np.eye(P, dtype=np.float32), "eye16": np.eye(P, dtype=np.float16),
    }
    arrays = {f"in_{k}": np.ascontiguousarray(v_) for k, v_ in arrays.items()}
    nc = bacc.Bacc("TRN2", target_bir_lowering=False, num_devices=1)
    aps = [nc.dram_tensor(k, v_.shape, mybir.dt.from_np(v_.dtype), kind="ExternalInput").ap() for k, v_ in arrays.items()]
    out = nc.dram_tensor("out", (B, S, D), F32, kind="ExternalOutput").ap()
    decoder(nc, *aps, out)
    r = run_bass_kernel_spmd(nc, [arrays], core_ids=[0])
    return r.results[0]["out"]
```
